# Optimizing a Trainium2 kernel written in Bass

```python
import numpy as np
import jax
import jax.numpy as jnp

def _softmax(x, axis=-1):
    return jax.nn.softmax(x, axis=axis)

def _gelu(x):
    return jax.nn.gelu(x, approximate=True)

def _silu(x):
    return jax.nn.silu(x)

def _sigmoid(x):
    return jax.nn.sigmoid(x)

def _layernorm(x, axis=-1, eps=1e-05):
    m = jnp.mean(x, axis=axis, keepdims=True)
    v = jnp.var(x, axis=axis, keepdims=True)
    return (x - m) / jnp.sqrt(v + eps)

def _scatter_add(tgt, idx, src, axis=0):
    return tgt.at[idx].add(src)

def _segment_sum(src, seg, n):
    return jax.ops.segment_sum(src, seg, n)
kernel_name = 'mk_prb_d1_jaxref_r8_28bbe6'

def setup_inputs(seed: int=0):
    np.random.seed(seed)
    _w = jnp.asarray

    def _L0_attn_setup():
        import jax, jax.numpy as jnp
        import numpy as np
        D_MODEL = 256
        NUM_HEADS = 16
        THETA = 10000.0

        def _rope(t, cos, sin):
            x_even = t[..., 0::2]
            x_odd = t[..., 1::2]
            rot = jnp.stack((-x_odd, x_even), axis=-1).reshape(t.shape)
            return t * cos + rot * sin
        key = jax.random.key(seed)
        ks = jax.random.split(key, 5)
        bs, S, d = (4, 256, D_MODEL)
        std = (2.0 / (d + d)) ** 0.5
        x = jax.random.normal(ks[0], (bs, S, d), dtype=jnp.float32)
        wq = jax.random.normal(ks[1], (d, d), dtype=jnp.float32) * std
        wk = jax.random.normal(ks[2], (d, d), dtype=jnp.float32) * std
        wv = jax.random.normal(ks[3], (d, d), dtype=jnp.float32) * std
        wo = jax.random.normal(ks[4], (d, d), dtype=jnp.float32) * std
        return {'x': x, 'wq': wq, 'wk': wk, 'wv': wv, 'wo': wo}
    _L0_attn_in = _L0_attn_setup()

    def _L0_ffn_setup():
        import jax, jax.numpy as jnp
        import numpy as np
        E, K, H, I = (64, 6, 256, 176)
        NS = 2
        IS = NS * I
        CAP = 32
        T_TOKENS = (1, 128)
        SCALE = 0.02

        def _moe_infer(x, gate_w, w_gate, w_up, w_down):
            T = x.shape[0]
            TK = T * K
            logits = x @ gate_w.T
            scores = jax.nn.softmax(logits, axis=-1)
            topk_w, topk_i = jax.lax.top_k(scores, K)
            flat_i = topk_i.reshape(-1)
            flat_w = topk_w.reshape(-1)
            token_ids = jnp.arange(TK, dtype=jnp.int32) // K
            order = jnp.argsort(flat_i)
            sorted_e = flat_i[order]
            counts = jnp.bincount(flat_i, length=E)
            starts = jnp.concatenate([jnp.zeros((1,), counts.dtype), jnp.cumsum(counts)[:-1]])
            pos_sorted = jnp.arange(TK) - starts[sorted_e]
            pos = jnp.zeros((TK,), jnp.int32).at[order].set(pos_sorted.astype(jnp.int32))
            valid = pos < CAP
            slot = jnp.where(valid, pos, CAP)
            buf = jnp.zeros((E, CAP + 1, H), x.dtype).at[flat_i, slot].set(x[token_ids])
            g = jnp.einsum('ech,ehi->eci', buf, w_gate)
            u = jnp.einsum('ech,ehi->eci', buf, w_up)
            y = jnp.einsum('eci,eih->ech', jax.nn.silu(g) * u, w_down)
            out_slots = y[flat_i, slot] * (flat_w * valid)[:, None]
            return out_slots.reshape(T, K, H).sum(axis=1)
        key = jax.random.key(seed)
        ks = jax.random.split(key, 8)
        f32 = jnp.float32
        return {'hidden_states': jax.random.normal(ks[0], (*T_TOKENS, H), f32), 'gate_w': jax.random.normal(ks[1], (E, H), f32) * SCALE, 'w_gate': jax.random.normal(ks[2], (E, H, I), f32) * SCALE, 'w_up': jax.random.normal(ks[3], (E, H, I), f32) * SCALE, 'w_down': jax.random.normal(ks[4], (E, I, H), f32) * SCALE, 'sw_gate': jax.random.normal(ks[5], (H, IS), f32) * SCALE, 'sw_up': jax.random.normal(ks[6], (H, IS), f32) * SCALE, 'sw_down': jax.random.normal(ks[7], (IS, H), f32) * SCALE}
    _L0_ffn_in = _L0_ffn_setup()
    _d = {'L0_attn_x': _L0_attn_in['x'], 'L0_attn_wq': _L0_attn_in['wq'], 'L0_attn_wk': _L0_attn_in['wk'], 'L0_attn_wv': _L0_attn_in['wv'], 'L0_attn_wo': _L0_attn_in['wo'], 'L0_ffn_gate_w': _L0_ffn_in['gate_w'], 'L0_ffn_w_gate': _L0_ffn_in['w_gate'], 'L0_ffn_w_up': _L0_ffn_in['w_up'], 'L0_ffn_w_down': _L0_ffn_in['w_down'], 'L0_ffn_sw_gate': _L0_ffn_in['sw_gate'], 'L0_ffn_sw_up': _L0_ffn_in['sw_up'], 'L0_ffn_sw_down': _L0_ffn_in['sw_down']}
    _x0 = _d['L0_attn_x']
    _d['L0_attn_x'] = jax.random.normal(jax.random.fold_in(jax.random.key(seed), 1), (4, 512, 256), dtype=_x0.dtype)
    del _x0
    return _d

def reference(L0_attn_x, L0_attn_wq, L0_attn_wk, L0_attn_wv, L0_attn_wo, L0_ffn_gate_w, L0_ffn_w_gate, L0_ffn_w_up, L0_ffn_w_down, L0_ffn_sw_gate, L0_ffn_sw_up, L0_ffn_sw_down):

    def _L0_attn_ref(x, wq, wk, wv, wo):
        import jax, jax.numpy as jnp
        import numpy as np
        D_MODEL = 256
        NUM_HEADS = 16
        THETA = 10000.0

        def _rope(t, cos, sin):
            x_even = t[..., 0::2]
            x_odd = t[..., 1::2]
            rot = jnp.stack((-x_odd, x_even), axis=-1).reshape(t.shape)
            return t * cos + rot * sin
        bs, S, d = x.shape
        H = NUM_HEADS
        dk = d // H
        q = (x @ wq.T).reshape(bs, S, H, dk).transpose(0, 2, 1, 3)
        k = (x @ wk.T).reshape(bs, S, H, dk).transpose(0, 2, 1, 3)
        v = (x @ wv.T).reshape(bs, S, H, dk).transpose(0, 2, 1, 3)
        half = dk // 2
        inv_freq = THETA ** (-2.0 * jnp.arange(half, dtype=jnp.float32) / dk)
        pos = jnp.arange(S, dtype=jnp.float32)
        ang = pos[:, None] * inv_freq[None, :]
        cos = jnp.repeat(jnp.cos(ang), 2, axis=-1)
        sin = jnp.repeat(jnp.sin(ang), 2, axis=-1)
        q = _rope(q, cos, sin)
        k = _rope(k, cos, sin)
        scale = 1.0 / jnp.sqrt(jnp.asarray(dk, dtype=x.dtype))
        attn = jnp.einsum('bhqd,bhkd->bhqk', q, k) * scale
        causal = jnp.tril(jnp.ones((S, S), dtype=bool))
        attn = jnp.where(causal, attn, -jnp.inf)
        probs = jax.nn.softmax(attn, axis=-1)
        out = jnp.einsum('bhqk,bhkd->bhqd', probs, v)
        out = out.transpose(0, 2, 1, 3).reshape(bs, S, d)
        return out @ wo.T

    def _L0_ffn_ref(hidden_states, gate_w, w_gate, w_up, w_down, sw_gate, sw_up, sw_down):
        import jax, jax.numpy as jnp
        import numpy as np
        E, K, H, I = (64, 6, 256, 176)
        NS = 2
        IS = NS * I
        CAP = 32
        T_TOKENS = (1, 128)
        SCALE = 0.02

        def _moe_infer(x, gate_w, w_gate, w_up, w_down):
            T = x.shape[0]
            TK = T * K
            logits = x @ gate_w.T
            scores = jax.nn.softmax(logits, axis=-1)
            topk_w, topk_i = jax.lax.top_k(scores, K)
            flat_i = topk_i.reshape(-1)
            flat_w = topk_w.reshape(-1)
            token_ids = jnp.arange(TK, dtype=jnp.int32) // K
            order = jnp.argsort(flat_i)
            sorted_e = flat_i[order]
            counts = jnp.bincount(flat_i, length=E)
            starts = jnp.concatenate([jnp.zeros((1,), counts.dtype), jnp.cumsum(counts)[:-1]])
            pos_sorted = jnp.arange(TK) - starts[sorted_e]
            pos = jnp.zeros((TK,), jnp.int32).at[order].set(pos_sorted.astype(jnp.int32))
            valid = pos < CAP
            slot = jnp.where(valid, pos, CAP)
            buf = jnp.zeros((E, CAP + 1, H), x.dtype).at[flat_i, slot].set(x[token_ids])
            g = jnp.einsum('ech,ehi->eci', buf, w_gate)
            u = jnp.einsum('ech,ehi->eci', buf, w_up)
            y = jnp.einsum('eci,eih->ech', jax.nn.silu(g) * u, w_down)
            out_slots = y[flat_i, slot] * (flat_w * valid)[:, None]
            return out_slots.reshape(T, K, H).sum(axis=1)
        orig_shape = hidden_states.shape
        x = hidden_states.reshape(-1, orig_shape[-1])
        y = _moe_infer(x, gate_w, w_gate, w_up, w_down).reshape(orig_shape)
        shared = jax.nn.silu(hidden_states @ sw_gate) * (hidden_states @ sw_up) @ sw_down
        return y + shared
    x = L0_attn_x
    xn = _layernorm(x, axis=-1)
    x = x + _L0_attn_ref(xn, L0_attn_wq, L0_attn_wk, L0_attn_wv, L0_attn_wo) + _L0_ffn_ref(xn, L0_ffn_gate_w, L0_ffn_w_gate, L0_ffn_w_up, L0_ffn_w_down, L0_ffn_sw_gate, L0_ffn_sw_up, L0_ffn_sw_down)
    return x

_drawn_inputs = setup_inputs


def setup_inputs(seed=0):
    import zlib

    import numpy as np

    out = dict(_drawn_inputs(seed))
    spreads = {}
    factors = {'L0_ffn_gate_w': 8.0,
     'L0_ffn_w_gate': 8.0,
     'L0_ffn_w_up': 8.0,
     'L0_ffn_w_down': 8.0,
     'L0_ffn_sw_gate': 2.924,
     'L0_ffn_sw_up': 2.894,
     'L0_ffn_sw_down': 2.888}
    for name, (base, spread) in spreads.items():
        noise = np.random.default_rng([zlib.crc32(name.encode()), seed]).standard_normal(out[name].shape)
        drawn = base * np.exp(spread * noise) if base else spread * noise
        out[name] = jnp.asarray(drawn.astype(out[name].dtype))
    for name, factor in factors.items():
        out[name] = (out[name] * factor).astype(out[name].dtype)
    return out
```

```python
from contextlib import ExitStack

import concourse.bass as bass
from concourse import mybir

ALU = mybir.AluOpType
ACT = mybir.ActivationFunctionType
AX = mybir.AxisListType
F32 = mybir.dt.float32
BF16 = mybir.dt.bfloat16
U32 = mybir.dt.uint32

P = 128
B, S, D = 4, 512, 256
T = B * S
NC = T // P
CB = S // P
H, DK = 16, 16
HB = P // DK
E, TOPK, CAP, I = 64, 6, 32, 176
IH = I // 2
IS = 2 * I
EG = P // CAP
NG = E // EG
NU = B * 2
NA = 2 * NU
NT = 6
KQ = NT * DK
KM = KQ + 3
EPS = 1e-5
BIG = 3.0e38
SM = [(0, 128), (128, 128), (256, 96)]
NDV = 2 + 3 * EG

C_ID, C_COS, C_SIN, C_BASE, C_OWN, C_PERM, C_TRI, C_M1, C_M2, C_IDS, C_END = (
    0, 128, 640, 1152, 1216, 1220, 1348, 1476, 1604, 1732, 1764)


def score_fills():
    first = [(qc, h, n) for qc, n in ((0, 4), (1, 2), (2, 1), (3, 1)) for h in range(0, 4, n)]
    second = [(kc, h, n) for kc, n in ((0, 1), (1, 1), (2, 2), (3, 4)) for h in range(0, 4, n)]
    return first, second


FIRST, SECOND = score_fills()
NF = len(FIRST)
PT_OFF = [0, 4 * 512, 4 * (512 + 384), 4 * (512 + 384 + 256)]
PT_W = 4 * (512 + 384 + 256 + 128)


def schedule():
    out = [("wT", i) for i in range(5)]
    for c in range(NC):
        out.append(("xT", c))
        if c >= 1:
            out.append(("lg", c - 1))
    out += [("lg", NC - 1), ("proj", 0), ("route", 0), ("pos", 0), ("pos", 1), ("slots", 0), ("disp", 0), ("wperm", 0)]
    for s in range(NA + 3):
        experts = [2 * (s - 1), 2 * (s - 1) + 1] if 1 <= s <= NG // 2 else []
        if s < NA + 2:
            out.append(("att", s))
        if s >= 3 and s % 2 == 1 and s < NA + 2:
            out.append(("norm", (s - 3) // 2))
        if s % 2 == 0 and s // 2 + 1 < NU:
            out.append(("proj", s // 2 + 1))
        if s < NA:
            out.append(("mT", s))
        if s % 4 == 1 and s < NA:
            out.append(("V", s // 4))
        for g in experts:
            out += [("xg", g), ("gu", g)]
            if g % 2 == 0 and 3 <= s < NA + 2 and s % 4 != 2:
                out.append(("sh", ((s - 3) // 4, (s - 3) % 4)))
            out += [("aT", g), ("dn", g)]
        if not experts and 3 <= s < NA + 2 and s % 4 != 2:
            out.append(("sh", ((s - 3) // 4, (s - 3) % 4)))
        if s >= 6 and s % 4 == 2:
            out += [("fin", s - 6 + i) for i in range(CB)]
        if 10 <= s < 18:
            out += [("comb", 2 * (s - 10)), ("comb", 2 * (s - 10) + 1)]
            if s < 16:
                out += [("store", 2 * (s - 10)), ("store", 2 * (s - 10) + 1)]
    out += [("store", c) for c in range(12, NC)]
    return out


SCHED = schedule()
RING = {"wT": (1, "act"), "xT": (1, "act"), "lg": (1, "act"), "pos": (1, "dve"), "disp": (1, "dve"), "wperm": (1, "act"),
        "proj": (4, "dve"), "V": (2, "act"), "mT": (1, "act"), "xg": (1, "act"), "gu": (1, "dve"),
        "aT": (1, "act"), "dn": (1, "act"), "sh": (2, "dve"), "fin": (1, "dve")}


def ring_counts():
    fill, emptied, count = {}, [], {"act": 0, "dve": 0}
    for stage in SCHED:
        if stage[0] in RING:
            fill[stage] = len(emptied)
            k, engine = RING[stage[0]]
            for _ in range(k):
                count[engine] += 1
                emptied.append((engine, count[engine]))
    return fill, emptied


FILL, EMPTIED = ring_counts()


def program(nc, x, wq, wk, wv, wo, gate_w, w_gate, w_up, w_down, sw_gate, sw_up, sw_down, const, out):
    xn_rows = nc.dram_tensor("xn_rows", (T, D), F32, kind="Internal").ap()
    y_rows = nc.dram_tensor("y_rows", (1 + E * CAP, D), F32, kind="Internal").ap()
    parts_d = nc.dram_tensor("parts_d", (2, 2, 3, DK, HB, S), BF16, kind="Internal").ap()

    with ExitStack() as ctx:
        def sb(name, shape, dt=F32):
            return ctx.enter_context(nc.sbuf_tensor(name, shape, dt))

        def bank(name):
            return ctx.enter_context(nc.psum_tensor(name, [P, 512], F32))

        def sem(name):
            return ctx.enter_context(nc.semaphore(name))

        cst = sb("cst", [P, C_END])
        cstb = sb("cstb", [P, C_END - C_TRI], BF16)
        identb = sb("identb", [P, P], BF16)
        onesb = sb("onesb", [P, P], BF16)
        onehat = sb("onehat", [P, 2, 32])
        graw = sb("graw", [E, D])
        wT = sb("wT", [P, 4, 2, D])
        wR = sb("wR", [P, 2, 2, D])
        gT = sb("gT", [P, 2, E])
        swg = sb("swg", [P, 2, IS])
        swu = sb("swu", [P, 2, IS])
        swd = sb("swd", [P, 3, D])
        acc = sb("acc", [P, NC, D])
        xnT = sb("xnT", [P, 2, T])
        st6 = sb("st6", [P, B, CB, 6])
        mv = sb("mv", [P, B, CB, 2])
        vareps = sb("vareps", [P, B, CB])
        std = sb("std", [P, B, CB])
        rstd = sb("rstd", [P, B, CB])
        newton = sb("newton", [P, CB])
        att_mem = sb("att_mem", [P, PT_W + CB * H * 32 + 2 * S + 3 * S])
        at = [0]

        def carve(n, dt=F32):
            lo = at[0]
            at[0] += n if dt == F32 else n // 2
            v = att_mem[:, lo:at[0]]
            return v if dt == F32 else v.bitcast(dt)

        L = carve(NC * (E + 2)).rearrange("p (c e) -> p c e", c=NC)
        Lrep = carve(NC * (E + 2)).rearrange("p (c e) -> p c e", c=NC)
        mask = carve(NC * E, BF16).rearrange("p (c e) -> p c e", c=NC)
        cum = carve(NC * E, BF16).rearrange("p (c e) -> p c e", c=NC)
        ex = carve(NC * E).rearrange("p (c e) -> p c e", c=NC)
        valid = carve(NC * E).rearrange("p (c e) -> p c e", c=NC)
        key = carve(NC * E).rearrange("p (c e) -> p c e", c=NC)
        pos1 = carve(NC * E, BF16).rearrange("p (c e) -> p c e", c=NC)
        disp = carve(NC * NG * NDV, BF16).rearrange("p (c g n) -> p c g n", c=NC, g=NG)
        at[0] = 0
        probs = carve(PT_W)
        vhat = carve(CB * H * 32).rearrange("p (c h w) -> p c h w", c=CB, h=H)
        aT = carve(2 * S).rearrange("p (k t) -> p k t", k=2)
        hT = carve(3 * S).rearrange("p (m t) -> p m t", m=3)
        top8 = sb("top8", [P, NC, 8])
        negtop = sb("negtop", [P, NC])
        exsum = sb("exsum", [P, NC])
        rsum = sb("rsum", [P, NC])
        slot8 = sb("slot8", [P, NC, 8])
        slotu = sb("slotu", [P, NC, 8], U32)
        got = sb("got", [P, NG, NDV])
        tokf = sb("tokf", [P, NG])
        toku = sb("toku", [P, NG], U32)
        w3 = sb("w3", [P, NG, EG])
        wgot = sb("wgot", [P, NG])
        wslot = sb("wslot", [P, NG])
        xg = sb("xg", [P, 4, D])
        xgT = sb("xgT", [P, 2, 2, P])
        wgu = sb("wgu", [P, 2, 2, EG, 2, I])
        wdn = sb("wdn", [P, 2, EG, 2, D])
        onehot = wdn[:, :, :, :, :].rearrange("p a e k d -> p (a e k d)").bitcast(BF16).rearrange(
            "p (n k e) -> p n k e", k=CAP, e=EG)
        th = sb("th", [P, I])
        ga = sb("ga", [P, I])
        hx = sb("hx", [P, I])
        hxT = sb("hxT", [IH, 2, P])
        ys = sb("ys", [P, 2, D])
        zrow = sb("zrow", [1, D])
        tsh = sb("tsh", [P, S])
        gsh = sb("gsh", [P, S])
        rots = sb("rots", [P, 2, 2, S])
        rot1, rot2 = rots[:, 0, :, :], rots[:, 1, :, :]
        xn = rots[:, :, :, :].rearrange("p a i s -> p (a i s)").rearrange("p (b c d) -> p b c d", b=2, c=CB)
        parts = sb("parts", [P, 2, 3, S], BF16)
        q6 = sb("q6", [P, 2, HB, S], BF16)
        k6 = sb("k6", [P, 2, HB, S], BF16)
        mx = sb("mx", [P, CB, 4])
        mres = sb("mres", [P, CB, 4])
        mp = sb("mp", [P, 2, CB, 3, 4], BF16)
        mrow = sb("mrow", [12, 2, S], BF16)
        recip = gsh
        wdn_flat = wdn[:, :, :, :, :].rearrange("p a e k d -> p (a e k d)")
        gb = wdn_flat[:, 0:2 * TOPK * D].rearrange("p (a k d) -> p a k d", a=2, k=TOPK)
        ysum = wdn_flat[:, 2 * TOPK * D:(2 * TOPK + 1) * D]
        wraw = wgu[:, :, :, :, :, :].rearrange("p a g e k i -> p (a g e k i)")[:, 0:8 * D].rearrange(
            "p (w o d) -> p w o d", w=4, o=2)

        pmax = [bank(f"pmax{i}") for i in range(2)]
        psc = [bank(f"psc{i}") for i in range(2)]
        pO = bank("pO")
        pD = bank("pD")
        ring = [bank(f"ring{i}") for i in range(2)]

        c_in = sem("c_in"); w_in = sem("w_in"); sw_in = sem("sw_in")
        x_in = [sem(f"x_in{b}") for b in range(B)]
        xn_out = [sem(f"xn_out{i}") for i in range(2)]
        const_b = sem("const_b"); pool_set = sem("pool_set"); rotw = sem("rotw")
        var_ready = sem("var_ready"); std_ready = sem("std_ready")
        xn_ready = sem("xn_ready")
        ring_full = sem("ring_full"); act_emptied = sem("act_emptied"); dve_emptied = sem("dve_emptied")
        mask_ready = sem("mask_ready"); negtop_ready = sem("negtop_ready"); ex_ready = sem("ex_ready")
        cum_ready = sem("cum_ready"); onehot_ready = sem("onehot_ready"); onehot_used = sem("onehot_used")
        slots_ready = sem("slots_ready"); tok_ready = sem("tok_ready")
        xg_in = [sem(f"xg_in{i}") for i in range(4)]
        wgu_in = [sem(f"wgu_in{i}") for i in range(2)]
        wdn_in = [sem(f"wdn_in{i}") for i in range(2)]
        tanh_ready = sem("tanh_ready"); hx_ready = sem("hx_ready")
        y_out = [sem(f"y_out{i}") for i in range(2)]
        z_out = sem("z_out")
        tsh_ready = sem("tsh_ready")
        rot_ready = sem("rot_ready"); parts_ready = sem("parts_ready")
        parts_out = sem("parts_out")
        qk_in = [sem(f"qk_in{i}") for i in range(2)]
        max_full = sem("max_full"); max_emptied = sem("max_emptied"); mp_ready = sem("mp_ready")
        m_in = [sem(f"m_in{i}") for i in range(2)]
        sc_full = sem("sc_full"); exp_done = sem("exp_done")
        pv_done = sem("pv_done"); norm_done = sem("norm_done")
        gb_in = [sem(f"gb_in{i}") for i in range(2)]
        gb_used = sem("gb_used"); acc_done = sem("acc_done"); out_done = sem("out_done")
        dve_chain = sem("dve_chain"); pool_chain = sem("pool_chain")

        def emptied(eng, stage, k=None):
            n = FILL[stage] + (RING[stage[0]][0] - 1 if k is None else k)
            engine, count = EMPTIED[n]
            eng.wait_ge(act_emptied if engine == "act" else dve_emptied, count)

        def filled(eng, stage, k=0):
            n = FILL[stage] + k
            eng.wait_ge(ring_full, n + 1)
            return ring[n % 2]

        order = {}
        for kind, arg in SCHED:
            order[(kind, arg)] = sum(1 for k2, _ in order if k2 == kind)

        ident = cst[:, C_ID:C_ID + P]
        tri = cstb[:, 0:P]
        mask_qk = cstb[:, P:2 * P]
        mask_kq = cstb[:, 2 * P:3 * P]
        ids = cstb[:, 3 * P:3 * P + 2 * NC].rearrange("p (c t) -> p c t", t=2)
        cosT = cst[:, C_COS:C_COS + S]
        sinT = cst[:, C_SIN:C_SIN + S]
        x_v = x.rearrange("b (c p) d -> b p c d", p=P)
        xn_v = xn_rows.rearrange("(b c p) d -> b p c d", p=P, c=CB)
        out_v = out.rearrange("b (c p) d -> b c p d", p=P)

        def acc_count(c, kind):
            n = 0
            for k2, a2 in SCHED:
                if k2 in ("fin", "comb"):
                    n += 1
                    if k2 == kind and a2 == c:
                        return n

        block = ctx.enter_context(nc.Block())

        @block.sync
        def _(sp):
            sp.dma_start(cst[:, :], const).then_inc(c_in, 16)
            for i, w in enumerate((wq, wk, wv, wo)):
                sp.dma_start(wraw[:, i, :, :], w.rearrange("(o p) d -> p o d", p=P)).then_inc(w_in, 16)
            sp.dma_start(graw[:, :], gate_w).then_inc(w_in, 16)
            for b in range(B):
                sp.dma_start(acc[:, CB * b:CB * b + CB, :], x_v[b]).then_inc(x_in[b], 16)
            sp.dma_start(swg[:, :, :], sw_gate.rearrange("(p k) i -> p k i", k=2)).then_inc(sw_in, 16)
            sp.dma_start(swu[:, :, :], sw_up.rearrange("(p k) i -> p k i", k=2)).then_inc(sw_in, 16)
            for m, (m0, mw) in enumerate(SM):
                sp.dma_start(swd[0:mw, m, :], sw_down[m0:m0 + mw, :]).then_inc(sw_in, 16)

            def load_experts(G):
                buf = G % 2
                if G >= 2:
                    emptied(sp, ("gu", G - 2))
                for i, w in enumerate((w_gate, w_up)):
                    sp.dma_start(wgu[:, buf, i, :, :, :].rearrange("p e k i -> p e (k i)"),
                                 w[EG * G:EG * G + EG].rearrange("e (p k) i -> p e (k i)", k=2)
                                 ).then_inc(wgu_in[buf], 16)
                if G >= 2:
                    emptied(sp, ("dn", G - 2))
                else:
                    sp.wait_ge(onehot_used, 4)
                sp.dma_start(wdn[0:IH, buf, :, :, :].rearrange("p e k d -> p e (k d)"),
                             w_down[EG * G:EG * G + EG].rearrange("e (p k) d -> p e (k d)", k=2)
                             ).then_inc(wdn_in[buf], 16)

            for kind, a in SCHED:
                if kind == "xT" and a % CB == 0:
                    b = a // CB
                    sp.wait_ge(xn_ready, CB * (b + 1))
                    sp.dma_start(xn_v[b], xn[:, b % 2, :, :]).then_inc(xn_out[b % 2], 16)
                elif kind == "disp":
                    load_experts(0)
                    load_experts(1)
                    sp.wait_ge(pool_set, 1)
                    sp.dma_start(y_rows[0:1, :], zrow[:, :]).then_inc(z_out, 16)
                elif kind == "proj":
                    buf = a % 2
                    sp.wait_ge(parts_ready, a + 1)
                    if a >= 2:
                        sp.wait_ge(qk_in[buf], 9 * 16 * (a // 2))
                    for i in range(2):
                        for t in range(3):
                            sp.dma_start(parts_d[buf, i, t].rearrange("d h n -> h d n"),
                                         parts[:, i, t, :]).then_inc(parts_out, 16)
                    sp.wait_ge(parts_out, 6 * 16 * (a + 1))
                    if a >= 2:
                        sp.wait_ge(sc_full, NF * (2 * a - 2))
                    for t, src in enumerate((0, 0, 0, 1, 1, 2)):
                        sp.dma_start(q6[DK * t:DK * t + DK, buf, :, :], parts_d[buf, 0, src]
                                     ).then_inc(qk_in[buf], 16)
                    for t0, n in ((0, 3), (3, 2), (5, 1)):
                        sp.dma_start(k6[DK * t0:DK * (t0 + n), buf, :, :],
                                     parts_d[buf, 1, 0:n].rearrange("t d h n -> (t d) h n")
                                     ).then_inc(qk_in[buf], 16)
                elif kind == "mT":
                    u, hg = a // 2, a % 2
                    emptied(sp, ("mT", a))
                    for t in range(3):
                        sp.dma_start(q6[KQ + t:KQ + t + 1, u % 2, hg::2, :], mrow[4 * t:4 * t + 4, a % 2, :]
                                     ).then_inc(m_in[a % 2], 16)
                elif kind == "dn":
                    emptied(sp, ("dn", a))
                    sp.dma_start(y_rows[1 + P * a:1 + P * a + P, :], ys[:, a % 2, :]).then_inc(y_out[a % 2], 16)
                    if a + 2 < NG:
                        load_experts(a + 2)
                elif kind == "store":
                    sp.wait_ge(acc_done, max(acc_count(a, "fin"), acc_count(a, "comb")))
                    sp.dma_start(out_v[a // CB, a % CB], acc[:, a, :]).then_inc(out_done, 16)
            sp.wait_ge(out_done, 16 * NC)

        @block.gpsimd
        def _(pool):
            links = [0]

            def link(ins):
                links[0] += 1
                ins.then_inc(pool_chain, 1)
                pool.wait_ge(pool_chain, links[0])

            nc.gpsimd.memset(zrow[:, :], 0.0).then_inc(pool_set, 1)
            nc.gpsimd.memset(onesb[:, :], 1.0).then_inc(pool_set, 1)
            link(nc.gpsimd.memset(onehat[:, :, :], 0.0))
            for i in range(2):
                nc.gpsimd.memset(onehat[:, i, DK * i:DK * i + DK], 1.0).then_inc(pool_set, 1)
            nc.gpsimd.memset(L[:, :, E:E + 2], BIG).then_inc(pool_set, 1)
            pool.wait_ge(pool_set, 5)
            nc.gpsimd.memset(k6[KQ:P, :, :, :], 1.0).then_inc(pool_set, 1)
            pool.wait_ge(pool_set, 6)
            nc.gpsimd.memset(cum[:, 0, :], 0.0).then_inc(pool_set, 1)
            def gather_tokens(G):
                if G >= 4:
                    emptied(pool, ("xg", G - 4))
                pool.indirect_dma_start(out=xg[:, G % 4, :], out_offset=None, in_=xn_rows,
                                        in_offset=bass.IndirectOffsetOnAxis(ap=toku[:, G:G + 1], axis=0)
                                        ).then_inc(xg_in[G % 4], 16)

            for kind, a in SCHED:
                if kind == "xT" and a == 1:
                    for i in range(2):
                        emptied(pool, ("wT", i))
                        for o in range(2):
                            nc.gpsimd.tensor_copy(wR[:, i, :, o::2], wT[:, i, :, 1 - o::2]).then_inc(rotw, 1)
                elif kind == "proj":
                    for i in range(2):
                        pool.wait_ge(rot_ready, 4 * a + 2 * i + 2)
                        if a >= 1 and i == 0:
                            pool.wait_ge(parts_out, 6 * 16 * a)
                        link(nc.gpsimd.tensor_add(rot1[:, i, :], rot1[:, i, :], rot2[:, i, :]))
                        link(nc.gpsimd.tensor_copy(parts[:, i, 0, :], rot1[:, i, :]))
                        link(nc.gpsimd.tensor_tensor(rot1[:, i, :], rot1[:, i, :], parts[:, i, 0, :],
                                                     ALU.subtract))
                        link(nc.gpsimd.tensor_copy(parts[:, i, 1, :], rot1[:, i, :]))
                        last = nc.gpsimd.tensor_tensor(parts[:, i, 2, :], rot1[:, i, :], parts[:, i, 1, :],
                                                       ALU.subtract)
                        if i == 0:
                            link(last)
                    last.then_inc(parts_ready, 1)
                elif kind == "disp":
                    pool.wait_ge(onehot_used, 4)
                    pool.wait_ge(tok_ready, 1)
                    nc.gpsimd.memset(vhat[:, :, :, :], 0.0).then_inc(pool_set, 1)
                    for i in range(2):
                        pool.wait_ge(xn_out[i], 32)
                    for G in range(4):
                        gather_tokens(G)
                elif kind == "xg" and a + 4 < NG:
                    gather_tokens(a + 4)
                elif kind == "comb":
                    if a == 0:
                        pool.wait_ge(slots_ready, 1)
                        pool.wait_ge(z_out, 16)
                        for i in range(2):
                            pool.wait_ge(y_out[i], 16 * (NG // 2))
                    if a >= 2:
                        pool.wait_ge(gb_used, a - 1)
                    for k in range(TOPK):
                        pool.indirect_dma_start(out=gb[:, a % 2, k, :], out_offset=None, in_=y_rows,
                                                in_offset=bass.IndirectOffsetOnAxis(
                                                    ap=slotu[:, a, k:k + 1], axis=0)
                                                ).then_inc(gb_in[a % 2], 16)

        @block.scalar
        def _(act):
            act.wait_ge(c_in, 16)
            nc.scalar.activation(cstb[:, :], cst[:, C_TRI:C_END], ACT.Copy).then_inc(const_b, 1)
            nc.scalar.activation(identb[:, :], ident, ACT.Copy).then_inc(const_b, 1)
            tanhs = 0
            for kind, a in SCHED:
                if kind == "wT":
                    r = filled(act, (kind, a))
                    if a < 4:
                        nc.scalar.activation(wT[:, a, :, :].rearrange("p k d -> p (k d)"), r[:, :],
                                             ACT.Copy).then_inc(act_emptied, 1)
                    else:
                        nc.scalar.activation(gT[:, :, :].rearrange("p k e -> p (k e)"), r[:, 0:2 * E],
                                             ACT.Copy).then_inc(act_emptied, 1)
                elif kind == "xT":
                    if a % CB == 0:
                        act.wait_ge(var_ready, a // CB + 1)
                        nc.scalar.activation(std[:, a // CB, :], vareps[:, a // CB, :], ACT.Sqrt
                                             ).then_inc(std_ready, 1)
                    r = filled(act, (kind, a))
                    nc.scalar.activation(xnT[:, :, P * a:P * a + P],
                                         r[:, 0:2 * P].rearrange("p (k t) -> p k t", k=2),
                                         ACT.Copy).then_inc(act_emptied, 1)
                elif kind == "lg":
                    r = filled(act, (kind, a))
                    nc.scalar.activation(L[:, a, 0:E], r[:, 0:E], ACT.Copy).then_inc(act_emptied, 1)
                elif kind == "pos" and a == 0:
                    act.wait_ge(negtop_ready, 1)
                    emptied(act, ("lg", NC - 1))
                    for c in range(NC):
                        nc.scalar.activation(ex[:, c, :], L[:, c, 0:E], ACT.Exp, bias=negtop[:, c:c + 1],
                                             accum_out=exsum[:, c:c + 1]).then_inc(ex_ready, 1)
                elif kind == "V":
                    if a == 0:
                        act.wait_ge(pool_set, 8)
                    else:
                        act.wait_ge(pv_done, CB * 4 * a)
                    for i in range(2):
                        r = filled(act, (kind, a), i)[:, :].rearrange("p (c h2 e d) -> p c h2 e d", c=2, e=2, d=DK)
                        vv = vhat[:, 2 * i:2 * i + 2, :, :].rearrange("p c (h2 e) w -> p c h2 e w", e=2)
                        for cc in range(2):
                            for e in range(2):
                                last = nc.scalar.activation(vv[:, cc, :, e, DK * e:DK * e + DK],
                                                            r[:, cc, :, e, :], ACT.Copy)
                        last.then_inc(act_emptied, 1)
                elif kind == "mT":
                    if a >= 2:
                        act.wait_ge(m_in[a % 2], 48 * (a // 2))
                    r = filled(act, (kind, a))
                    nc.scalar.activation(mrow[:, a % 2, :], r[:, :].bitcast(BF16)[0:12, 0:S],
                                         ACT.Copy).then_inc(act_emptied, 1)
                elif kind == "att" and 1 <= a <= NA:
                    g = a - 1
                    for i, (kc, h0, n) in enumerate(SECOND):
                        act.wait_ge(sc_full, NF * g + i + 1)
                        if g >= 1:
                            act.wait_ge(pv_done, CB * (g - 1) + kc + 1)
                        w = S - P * kc
                        o = PT_OFF[kc] + h0 * w
                        nc.scalar.activation(probs[:, o:o + n * w], psc[(NF * g + i) % 2][:, 0:n * w],
                                             ACT.Exp, scale=DK ** -0.5).then_inc(exp_done, 1)
                elif kind == "xg":
                    r = filled(act, (kind, a))
                    if a >= 2:
                        emptied(act, ("gu", a - 2))
                    nc.scalar.activation(xgT[:, a % 2, :, :].rearrange("p k t -> p (k t)"), r[:, 0:2 * P],
                                         ACT.Copy).then_inc(act_emptied, 1)
                elif kind == "gu":
                    r = filled(act, (kind, a))
                    if a >= 1:
                        emptied(act, ("gu", a - 1))
                    nc.scalar.activation(th[:, :], r[:, 0:I], ACT.Tanh, scale=0.5).then_inc(tanh_ready, 1)
                elif kind == "aT":
                    r = filled(act, (kind, a))
                    nc.scalar.activation(hxT[:, :, :].rearrange("p k t -> p (k t)"), r[0:IH, 0:2 * P],
                                         ACT.Copy).then_inc(act_emptied, 1)
                elif kind == "wperm":
                    r = filled(act, (kind, a))
                    nc.scalar.activation(wslot[:, :], r[:, 0:NG], ACT.Copy).then_inc(act_emptied, 1)
                elif kind == "dn":
                    r = filled(act, (kind, a))
                    if a == 0:
                        emptied(act, ("wperm", 0))
                    if a >= 2:
                        act.wait_ge(y_out[a % 2], 16 * (a // 2))
                    nc.scalar.activation(ys[:, a % 2, :], r[:, 0:D], ACT.Copy,
                                         scale=wslot[:, a:a + 1]).then_inc(act_emptied, 1)
                elif kind == "sh":
                    m0, mw = SM[a[1]]
                    r = filled(act, (kind, a), 0)
                    tanhs += 1
                    if tanhs >= 2:
                        emptied(act, last_sh)
                    last_sh = (kind, a)
                    nc.scalar.activation(tsh[0:mw, :], r[0:mw, :], ACT.Tanh, scale=0.5).then_inc(tsh_ready, 1)

        @block.vector
        def _(dve):
            links = [0]

            def link(ins):
                links[0] += 1
                ins.then_inc(dve_chain, 1)
                dve.wait_ge(dve_chain, links[0])

            def variances(b):
                dve.wait_ge(x_in[b], 16)
                for c in range(CB):
                    last = nc.vector.bn_stats(st6[:, b, c, :], acc[:, CB * b + c, :])
                link(last)
                for c in range(CB):
                    last = nc.vector.bn_aggr(mv[:, b, c, :], st6[:, b, c, :])
                link(last)
                nc.vector.tensor_scalar(vareps[:, b, :], mv[:, b, :, 1], EPS, None, ALU.add).then_inc(var_ready, 1)

            shs = 0
            for kind, a in SCHED:
                if kind == "xT" and a % CB == 0:
                    b = a // CB
                    if b == 0:
                        variances(0)
                    if b < B - 1:
                        variances(b + 1)
                    dve.wait_ge(std_ready, b + 1)
                    link(nc.vector.reciprocal(rstd[:, b, :], std[:, b, :]))
                    link(nc.vector.tensor_tensor(newton[:, :], vareps[:, b, :], rstd[:, b, :], ALU.mult))
                    link(nc.vector.tensor_tensor(newton[:, :], newton[:, :], rstd[:, b, :], ALU.mult))
                    link(nc.vector.tensor_scalar(newton[:, :], newton[:, :], -0.5, 1.5, ALU.mult, ALU.add))
                    link(nc.vector.tensor_tensor(rstd[:, b, :], rstd[:, b, :], newton[:, :], ALU.mult))
                    if b >= 2:
                        dve.wait_ge(xn_out[b % 2], 16 * (b // 2))
                        emptied(dve, ("xT", CB * (b - 1) - 1))
                    for c in range(CB):
                        nc.vector.tensor_scalar(xn[:, b % 2, c, :], acc[:, CB * b + c, :], mv[:, b, c, 0:1],
                                                rstd[:, b, c:c + 1], ALU.subtract, ALU.mult).then_inc(xn_ready, 1)
                elif kind == "route":
                    emptied(dve, ("lg", NC - 1))
                    dve.wait_ge(pool_set, 7)
                    for c in range(NC):
                        last = nc.vector.max(top8[:, c, :], L[:, c, :])
                    link(last)
                    nc.vector.tensor_scalar(negtop[:, :], top8[:, :, 2], -1.0, None, ALU.mult).then_inc(negtop_ready, 1)
                    for c in range(NC):
                        last = nc.vector.match_replace(Lrep[:, c, :], top8[:, c, :], L[:, c, :], -BIG)
                    link(last)
                    nc.vector.tensor_tensor(mask[:, :, :], L[:, :, 0:E], Lrep[:, :, 0:E], ALU.is_gt
                                            ).then_inc(mask_ready, 1)
                    dve.wait_ge(mask_ready, 1)
                    for c in range(1, NC):
                        nc.vector.tensor_tensor(cum[:, c, :], cum[:, c - 1, :], mask[:, c - 1, :], ALU.add
                                                ).then_inc(cum_ready, 1)
                        dve.wait_ge(cum_ready, c)
                elif kind == "pos":
                    r = filled(dve, (kind, a))[:, :].rearrange("p (c e) -> p c e", e=E)
                    cs = slice(8 * a, 8 * a + 8)
                    base = cst[:, C_BASE:C_BASE + E].rearrange("p (o e) -> p o e", o=1).broadcast_to([P, 8, E])
                    link(nc.vector.scalar_tensor_tensor(valid[:, cs, :], r, float(CAP), mask[:, cs, :],
                                                        ALU.is_lt, ALU.mult))
                    nc.vector.tensor_tensor(key[:, cs, :], r, base, ALU.add)
                    nc.vector.scalar_tensor_tensor(pos1[:, cs, :], r, 1.0, valid[:, cs, :],
                                                   ALU.add, ALU.mult).then_inc(dve_emptied, 1)
                    emptied(dve, (kind, a))
                    link(nc.vector.tensor_tensor(key[:, cs, :], key[:, cs, :], valid[:, cs, :], ALU.mult))
                elif kind == "slots":
                    for c in range(NC):
                        last = nc.vector.max(slot8[:, c, :], key[:, c, :])
                    link(last)
                    nc.vector.tensor_copy(slotu[:, :, :], slot8[:, :, :]).then_inc(slots_ready, 1)
                    dve.wait_ge(ex_ready, NC)
                    link(nc.vector.reciprocal(rsum[:, :], exsum[:, :]))
                    rb = rsum[:, :].rearrange("p (c o) -> p c o", o=1).broadcast_to([P, NC, E])
                    link(nc.vector.tensor_tensor(ex[:, :, :], ex[:, :, :], rb, ALU.mult))
                    exg = ex[:, :, :].rearrange("p c (g e) -> p (c g) e", e=EG)
                    dg = disp[:, :, :, :].rearrange("p c g n -> p (c g) n")
                    part = [dg[:, :, 2 + EG * t:2 + EG * t + EG] for t in range(3)]
                    link(nc.vector.tensor_copy(part[0], exg))
                    link(nc.vector.tensor_tensor(exg, exg, part[0], ALU.subtract))
                    link(nc.vector.tensor_copy(part[1], exg))
                    link(nc.vector.tensor_tensor(part[2], exg, part[1], ALU.subtract))
                    idb = ids.rearrange("p c (o t) -> p c o t", o=1).broadcast_to([P, NC, NG, 2])
                    dve.wait_ge(const_b, 1)
                    link(nc.vector.tensor_copy(disp[:, :, :, 0:2], idb))
                elif kind == "disp":
                    for part in range(4):
                        if part:
                            dve.wait_ge(onehot_used, part)
                        src = pos1[:, 4 * part:4 * part + 4, :].rearrange("p c (g e) -> p (c g) e", e=EG)
                        for k in range(CAP):
                            last = nc.vector.tensor_scalar(onehot[:, :, k, :], src, float(k + 1), None, ALU.is_equal)
                        last.then_inc(onehot_ready, 1)
                    r = filled(dve, (kind, a))
                    nc.vector.tensor_copy(got[:, :, :].rearrange("p g n -> p (g n)"), r[:, 0:NG * NDV]
                                          ).then_inc(dve_emptied, 1)
                    emptied(dve, (kind, a))
                    link(nc.vector.scalar_tensor_tensor(tokf[:, :], got[:, :, 0], float(P), got[:, :, 1],
                                                        ALU.mult, ALU.add))
                    nc.vector.tensor_copy(toku[:, :], tokf[:, :]).then_inc(tok_ready, 1)
                    link(nc.vector.tensor_tensor(w3[:, :, :], got[:, :, 2:2 + EG], got[:, :, 2 + EG:2 + 2 * EG], ALU.add))
                    link(nc.vector.tensor_tensor(w3[:, :, :], w3[:, :, :], got[:, :, 2 + 2 * EG:NDV], ALU.add))
                    own = cst[:, C_OWN:C_OWN + EG].rearrange("p (o e) -> p o e", o=1).broadcast_to([P, NG, EG])
                    link(nc.vector.tensor_tensor(w3[:, :, :], w3[:, :, :], own, ALU.mult))
                    nc.vector.tensor_reduce(wgot[:, :], w3[:, :, :], AX.X, ALU.add).then_inc(tok_ready, 1)
                elif kind == "proj":
                    if a == 0:
                        dve.wait_ge(c_in, 16)
                        for i in range(2):
                            dve.wait_ge(xn_out[i], 32)
                        emptied(dve, ("xT", NC - 1))
                    for i in range(2):
                        if a >= 1 and i == 0:
                            dve.wait_ge(parts_ready, a)
                        for j, (dst, tab) in enumerate(((rot1, cosT), (rot2, sinT))):
                            r = filled(dve, (kind, a), 2 * i + j)
                            dve_i = nc.vector.tensor_tensor(dst[:, i, :], r[:, :], tab, ALU.mult)
                            dve_i.then_inc(dve_emptied, 1)
                        emptied(dve, (kind, a), 2 * i + 1)
                        dve.sem_inc(rot_ready, 2)
                elif kind == "att" and a < NA:
                    for i, (qc, h0, n) in enumerate(FIRST):
                        w = P * (qc + 1)
                        dve.wait_ge(max_full, NF * a + i + 1)
                        r = pmax[(NF * a + i) % 2][:, 0:n * w].rearrange("p (h w) -> p h w", h=n)
                        nc.vector.tensor_reduce(mx[:, qc, h0:h0 + n], r, AX.X, ALU.max).then_inc(max_emptied, 1)
                    dve.wait_ge(max_emptied, NF * (a + 1))
                    if a >= 2:
                        emptied(dve, ("mT", a - 2))
                    m = mp[:, a % 2, :, :, :]
                    link(nc.vector.tensor_scalar(m[:, :, 0, :], mx[:, :, :], -1.0, None, ALU.mult))
                    link(nc.vector.scalar_tensor_tensor(mres[:, :, :], mx[:, :, :], -1.0, m[:, :, 0, :],
                                                        ALU.mult, ALU.subtract))
                    link(nc.vector.tensor_copy(m[:, :, 1, :], mres[:, :, :]))
                    nc.vector.tensor_tensor(m[:, :, 2, :], mres[:, :, :], m[:, :, 1, :],
                                            ALU.subtract).then_inc(mp_ready, 1)
                    dve.wait_ge(mp_ready, a + 1)
                elif kind == "gu":
                    r = filled(dve, (kind, a))
                    dve.wait_ge(tanh_ready, a + 1)
                    if a >= 1:
                        emptied(dve, ("aT", a - 1))
                    link(nc.vector.scalar_tensor_tensor(ga[:, :], th[:, :], 1.0, r[:, 0:I], ALU.add, ALU.mult))
                    nc.vector.scalar_tensor_tensor(hx[:, :], ga[:, :], 0.5, r[:, I:2 * I], ALU.mult, ALU.mult
                                                   ).then_inc(dve_emptied, 1)
                    emptied(dve, (kind, a))
                elif kind == "sh":
                    b, m = a
                    mw = SM[m][1]
                    shs += 1
                    dve.wait_ge(tsh_ready, shs)
                    r = filled(dve, (kind, a), 0)
                    nc.vector.scalar_tensor_tensor(gsh[0:mw, :], tsh[0:mw, :], 1.0, r[0:mw, :], ALU.add, ALU.mult
                                                   ).then_inc(dve_emptied, 1)
                    emptied(dve, (kind, a), 0)
                    if b >= 1 and m == 0:
                        emptied(dve, ("fin", CB * b - 1))
                    r = filled(dve, (kind, a), 1)
                    nc.vector.scalar_tensor_tensor(hT[0:mw, m, :], gsh[0:mw, :], 0.5, r[0:mw, :],
                                                   ALU.mult, ALU.mult).then_inc(dve_emptied, 1)
                    emptied(dve, (kind, a), 1)
                elif kind == "norm":
                    b, blk = a // 2, a % 2
                    dve.wait_ge(pv_done, CB * (2 * a + 2))
                    if b >= 1 and blk == 0:
                        emptied(dve, ("fin", CB * b - 1))
                    link(nc.vector.reciprocal(recip[:, :], pD[:, :]))
                    nc.vector.tensor_tensor(aT[:, blk, :], pO[:, :], recip[:, :], ALU.mult
                                            ).then_inc(norm_done, 1)
                    dve.wait_ge(norm_done, a + 1)
                elif kind == "fin":
                    r = filled(dve, (kind, a))
                    dve.wait_ge(xn_ready, NC)
                    link(nc.vector.tensor_tensor(acc[:, a, :], acc[:, a, :], r[:, 0:D], ALU.add))
                    dve.sem_inc(dve_emptied, 1)
                    dve.sem_inc(acc_done, 1)
                elif kind == "comb":
                    dve.wait_ge(gb_in[a % 2], TOPK * 16 * (a // 2 + 1))
                    nc.vector.tensor_reduce(ysum[:, :], gb[:, a % 2, :, :].rearrange("p k d -> p d k"), AX.X,
                                            ALU.add).then_inc(gb_used, 1)
                    dve.wait_ge(gb_used, a + 1)
                    link(nc.vector.tensor_tensor(acc[:, a, :], acc[:, a, :], ysum[:, :], ALU.add))
                    dve.sem_inc(acc_done, 1)

        @block.tensor
        def _(pe):
            def claim(stage, k=0):
                n = FILL[stage] + k
                if n >= 2:
                    engine, count = EMPTIED[n - 2]
                    pe.wait_ge(act_emptied if engine == "act" else dve_emptied, count)
                return ring[n % 2]

            def scores_for_max(g, i):
                u, hg = g // 2, g % 2
                qc, h0, n = FIRST[i]
                f = NF * g + i
                if f >= 2:
                    pe.wait_ge(max_emptied, f - 1)
                w = P * (qc + 1)
                for j in range(n):
                    h = 2 * (h0 + j) + hg
                    o = pmax[f % 2][:, w * j:w * j + w]
                    nc.tensor.matmul(o, q6[0:KQ, u % 2, h, P * qc:P * qc + P], k6[0:KQ, u % 2, h, 0:w],
                                     start=True, stop=False)
                    last = nc.tensor.matmul(o[:, w - P:w], identb[:, :], mask_qk, start=False, stop=True)
                last.then_inc(max_full, 1)

            def scores_for_exp(g, i):
                u, hg = g // 2, g % 2
                kc, h0, n = SECOND[i]
                f = NF * g + i
                if f >= 2:
                    pe.wait_ge(exp_done, f - 1)
                w = S - P * kc
                for j in range(n):
                    h = 2 * (h0 + j) + hg
                    o = psc[f % 2][:, w * j:w * j + w]
                    nc.tensor.matmul(o, k6[0:KM, u % 2, h, P * kc:P * kc + P], q6[0:KM, u % 2, h, P * kc:S],
                                     start=True, stop=False)
                    last = nc.tensor.matmul(o[:, 0:P], identb[:, :], mask_kq, start=False, stop=True)
                last.then_inc(sc_full, 1)

            def values_begin(g):
                u = g // 2
                emptied(pe, ("V", u // 2))
                if g % 2 == 0 and u >= 1:
                    pe.wait_ge(norm_done, u)

            def values(g, kc, which):
                u, hg = g // 2, g % 2
                w = S - P * kc
                for n in which:
                    j = n % 4
                    if n == 0:
                        pe.wait_ge(exp_done, NF * g + max(i for i in range(NF) if SECOND[i][0] == kc) + 1)
                    v = vhat[:, kc, HB * (u % 2) + 2 * j + hg, :] if n < 4 else onehat[:, hg, :]
                    dst = pO if n < 4 else pD
                    o = PT_OFF[kc] + w * j
                    last = nc.tensor.matmul(dst[32 * j:32 * j + 32, P * kc:S], v, probs[:, o:o + w],
                                            start=(hg == 0 and kc == 0), stop=(hg == 1 and kc == CB - 1),
                                            skip_group_check=True)
                    if n == 7:
                        last.then_inc(pv_done, 1)

            pe.wait_ge(c_in, 16)
            pe.wait_ge(w_in, 5 * 16)
            for kind, a in SCHED:
                if kind == "wT":
                    r = claim((kind, a))
                    for k in range(2):
                        if a == 4:
                            last = nc.tensor.transpose(r[:, E * k:E * k + E], graw[:, k::2], ident[0:E, 0:E])
                            continue
                        for o in range(2):
                            src = wraw[:, a, o, k::2] if a < 3 else wraw[:, a, o, P * k:P * k + P]
                            last = nc.tensor.transpose(r[:, D * k + P * o:D * k + P * o + P], src, ident)
                    last.then_inc(ring_full, 1)
                elif kind == "xT":
                    r = claim((kind, a))
                    pe.wait_ge(xn_ready, a + 1)
                    for k in range(2):
                        last = nc.tensor.transpose(r[:, P * k:P * k + P], xn[:, a // CB % 2, a % CB, k::2], ident)
                    last.then_inc(ring_full, 1)
                elif kind == "lg":
                    r = claim((kind, a))
                    emptied(pe, ("xT", a))
                    for k in range(2):
                        last = nc.tensor.matmul(r[:, 0:E], xnT[:, k, P * a:P * a + P], gT[:, k, :],
                                                start=(k == 0), stop=(k == 1))
                    last.then_inc(ring_full, 1)
                elif kind == "pos":
                    r = claim((kind, a))
                    pe.wait_ge(const_b, 2)
                    pe.wait_ge(pool_set, 2)
                    pe.wait_ge(cum_ready, NC - 1)
                    for c in range(8 * a, 8 * a + 8):
                        o = r[:, E * (c % 8):E * (c % 8) + E]
                        nc.tensor.matmul(o, tri, mask[:, c, :], start=True, stop=False)
                        last = nc.tensor.matmul(o, onesb[:, :], cum[:, c, :], start=False, stop=True)
                    last.then_inc(ring_full, 1)
                elif kind == "disp":
                    r = claim((kind, a))
                    for part in range(4):
                        pe.wait_ge(onehot_ready, part + 1)
                        for c in range(4 * part, 4 * part + 4):
                            for G in range(NG):
                                last = nc.tensor.matmul(
                                    r[:, NDV * G:NDV * G + NDV],
                                    onehot[:, (c % 4) * NG + G, :, :].rearrange("p k e -> p (k e)"), disp[:, c, G, :],
                                    start=(c == 0 and G == 0), stop=(c == NC - 1), skip_group_check=True)
                        if part < 3:
                            last.then_inc(onehot_used, 1)
                    last.then_inc(onehot_used, 1)
                    pe.wait_ge(onehot_used, 4)
                    pe.sem_inc(ring_full, 1)
                elif kind == "wperm":
                    r = claim((kind, a))
                    pe.wait_ge(tok_ready, 2)
                    nc.tensor.matmul(r[:, 0:NG], cst[:, C_PERM:C_PERM + P], wgot[:, :], start=True, stop=True
                                     ).then_inc(ring_full, 1)
                elif kind == "proj":
                    b, blk = a // 2, a % 2
                    if a == 0:
                        pe.wait_ge(rotw, 4)
                    emptied(pe, ("xT", CB * (b + 1) - 1))
                    for i in range(2):
                        for j, w in enumerate((wT, wR)):
                            r = claim((kind, a), 2 * i + j)
                            for k in range(2):
                                last = nc.tensor.matmul(r[:, :], w[:, i, k, P * blk:P * blk + P],
                                                        xnT[:, k, S * b:S * b + S], start=(k == 0), stop=(k == 1))
                            last.then_inc(ring_full, 1)
                elif kind == "V":
                    for i in range(2):
                        r = claim((kind, a), i)
                        for cc in range(2):
                            c = CB * a + 2 * i + cc
                            for k in range(2):
                                last = nc.tensor.matmul(r[:, D * cc:D * cc + D], xnT[:, k, P * c:P * c + P],
                                                        wT[:, 2, k, :], start=(k == 0), stop=(k == 1))
                        last.then_inc(ring_full, 1)
                elif kind == "sh":
                    b, m = a
                    m0, mw = SM[m]
                    pe.wait_ge(sw_in, 5 * 16)
                    for i, w in enumerate((swg, swu)):
                        r = claim((kind, a), i)
                        for k in range(2):
                            last = nc.tensor.matmul(r[0:mw, :], w[:, k, m0:m0 + mw], xnT[:, k, S * b:S * b + S],
                                                    start=(k == 0), stop=(k == 1))
                        last.then_inc(ring_full, 1)
                elif kind == "att":
                    if a < NA:
                        pe.wait_ge(qk_in[a // 2 % 2], 9 * 16 * (a // 4 + 1))
                    if 1 <= a <= NA:
                        pe.wait_ge(m_in[(a - 1) % 2], 48 * ((a - 1) // 2 + 1))
                    if a == 1:
                        pe.wait_ge(pool_set, 6)
                    if a >= 2:
                        values_begin(a - 2)
                        values(a - 2, 0, range(8))
                    for i in range(NF):
                        if a < NA:
                            scores_for_max(a, i)
                        if 1 <= a <= NA:
                            scores_for_exp(a - 1, i)
                        if a >= 2 and i < 8:
                            values(a - 2, 1 + i // 4, range(2 * (i % 4), 2 * (i % 4) + 2))
                        elif a >= 2 and i < 10:
                            values(a - 2, 3, range(4 * (i - 8), 4 * (i - 8) + 4))
                elif kind == "mT":
                    r = claim((kind, a))
                    pe.wait_ge(mp_ready, a + 1)
                    for qc in range(CB):
                        last = nc.tensor.transpose(r[:, :].bitcast(BF16)[0:12, P * qc:P * qc + P],
                                                   mp[:, a % 2, qc, :, :].rearrange("p t h -> p (t h)"), identb[:, :])
                    last.then_inc(ring_full, 1)
                elif kind == "xg":
                    r = claim((kind, a))
                    pe.wait_ge(xg_in[a % 4], 16 * (a // 4 + 1))
                    for k in range(2):
                        last = nc.tensor.transpose(r[:, P * k:P * k + P], xg[:, a % 4, k::2], ident)
                    last.then_inc(ring_full, 1)
                elif kind == "gu":
                    r = claim((kind, a))
                    pe.wait_ge(wgu_in[a % 2], 32 * (a // 2 + 1))
                    emptied(pe, ("xg", a))
                    for k in range(2):
                        for j in range(EG):
                            last = nc.tensor.matmul(r[32 * j:32 * j + 32, 0:2 * I],
                                                    xgT[:, a % 2, k, j::EG],
                                                    wgu[:, a % 2, :, j, k, :], start=(k == 0), stop=(k == 1))
                    last.then_inc(ring_full, 1)
                elif kind == "aT":
                    r = claim((kind, a))
                    emptied(pe, ("gu", a))
                    if a >= 1:
                        emptied(pe, ("dn", a - 1))
                    for k in range(2):
                        last = nc.tensor.transpose(r[0:IH, P * k:P * k + P], hx[:, k::2], ident)
                    last.then_inc(ring_full, 1)
                elif kind == "dn":
                    r = claim((kind, a))
                    pe.wait_ge(wdn_in[a % 2], 16 * (a // 2 + 1))
                    emptied(pe, ("aT", a))
                    for k in range(2):
                        for j in range(EG):
                            last = nc.tensor.matmul(r[32 * j:32 * j + 32, 0:D], hxT[:, k, CAP * j:CAP * j + CAP],
                                                    wdn[0:IH, a % 2, j, k, :], start=(k == 0), stop=(k == 1))
                    last.then_inc(ring_full, 1)
                elif kind == "fin":
                    b, cq = a // CB, a % CB
                    r = claim((kind, a))
                    pe.wait_ge(norm_done, 2 * b + 2)
                    emptied(pe, ("sh", (b, 2)), 1)
                    for blk in range(2):
                        nc.tensor.matmul(r[:, 0:D], aT[:, blk, P * cq:P * cq + P], wT[:, 3, blk, :],
                                         start=(blk == 0), stop=False)
                    for m, (m0, mw) in enumerate(SM):
                        last = nc.tensor.matmul(r[:, 0:D], hT[0:mw, m, P * cq:P * cq + P], swd[0:mw, m, :],
                                                start=False, stop=(m == 2))
                    last.then_inc(ring_full, 1)


def constants(np):
    f = np.float32
    c = np.zeros((P, C_END), f)
    c[:, C_ID:C_ID + P] = np.eye(P, dtype=f)
    inv = f(10000.0) ** (f(-2.0) * np.arange(DK // 2, dtype=f) / f(DK))
    ang = (np.arange(S, dtype=f)[:, None] * inv[None, :].astype(f)).astype(f)
    row = (np.arange(P) % DK) // 2
    sign = np.where(np.arange(P) % 2 == 0, f(-1), f(1))
    c[:, C_COS:C_COS + S] = np.cos(ang).T[row]
    c[:, C_SIN:C_SIN + S] = np.sin(ang).T[row] * sign[:, None]
    c[:, C_BASE:C_BASE + E] = (CAP * np.arange(E) + 1)[None, :]
    p = np.arange(P)
    c[:, C_OWN:C_OWN + EG] = p[:, None] % EG == np.arange(EG)[None, :]
    c[p, C_PERM + p % EG * CAP + p // EG] = 1
    c[:, C_TRI:C_TRI + P] = p[:, None] < p[None, :]
    c[:, C_M1:C_M1 + P] = np.where(p[None, :] > p[:, None], f(-1e30), f(0))
    c[:, C_M2:C_M2 + P] = np.where(p[:, None] > p[None, :], f(-1e30), f(0))
    c[:, C_IDS:C_IDS + 2 * NC:2] = np.arange(NC)[None, :]
    c[:, C_IDS + 1:C_IDS + 2 * NC:2] = p[:, None]
    return c


_INS = ["L0_attn_x", "L0_attn_wq", "L0_attn_wk", "L0_attn_wv", "L0_attn_wo", "L0_ffn_gate_w", "L0_ffn_w_gate",
        "L0_ffn_w_up", "L0_ffn_w_down", "L0_ffn_sw_gate", "L0_ffn_sw_up", "L0_ffn_sw_down"]


def kernel(**inputs):
    import numpy as _np
    import concourse.bacc as _bacc
    from concourse.bass_utils import run_bass_kernel_spmd as _run

    nc = _bacc.Bacc("TRN2", target_bir_lowering=False, num_devices=1)
    arrays, args = {}, []
    for name in _INS + ["const"]:
        a = constants(_np) if name == "const" else _np.ascontiguousarray(inputs[name])
        arrays[f"in_{name}"] = a
        args.append(nc.dram_tensor(f"in_{name}", a.shape, F32, kind="ExternalInput").ap())
    out = nc.dram_tensor("out0", (B, S, D), F32, kind="ExternalOutput").ap()
    program(nc, *args, out)
    r = _run(nc, [arrays], core_ids=[0])
    return r.results[0]["out0"]
```

```python
from contextlib import ExitStack

import concourse.bass as bass
from concourse import mybir

ALU = mybir.AluOpType
ACT = mybir.ActivationFunctionType
AX = mybir.AxisListType
F32 = mybir.dt.float32
BF16 = mybir.dt.bfloat16
U32 = mybir.dt.uint32

P = 128
B, S, D = 4, 512, 256
T = B * S
NC = T // P
CB = S // P
H, DK = 16, 16
HB = P // DK
E, TOPK, CAP, I = 64, 6, 32, 176
IH = I // 2
IS = 2 * I
EG = P // CAP
NG = E // EG
NU = B * 2
NA = 2 * NU
NT = 6
KQ = NT * DK
KM = KQ + 3
EPS = 1e-5
BIG = 3.0e38
SM = [(0, 128), (128, 128), (256, 96)]
NDV = 2 + 3 * EG

C_ID, C_COS, C_SIN, C_BASE, C_OWN, C_PERM, C_TRI, C_M1, C_M2, C_IDS, C_END = (
    0, 128, 640, 1152, 1216, 1220, 1348, 1476, 1604, 1732, 1764)


def score_fills():
    first = [(qc, h, n) for qc, n in ((0, 4), (1, 2), (2, 1), (3, 1)) for h in range(0, 4, n)]
    second = [(kc, h, n) for kc, n in ((0, 1), (1, 1), (2, 2), (3, 4)) for h in range(0, 4, n)]
    return first, second


FIRST, SECOND = score_fills()
NF = len(FIRST)
PT_OFF = [0, 4 * 512, 4 * (512 + 384), 4 * (512 + 384 + 256)]
PT_W = 4 * (512 + 384 + 256 + 128)


MAX_Q = ((0, 1, 2), (3, 4, 5), (6, 7, 8), (9, 10))
EXP_Q = ((), (0, 1, 2), (3, 4, 5, 6), (7, 8, 9, 10))


def schedule():
    out = [("ln", 0)] + [("wT", i) for i in range(5)] + [("xT", c) for c in range(CB)] + [("ln", 1), ("proj", 0)]
    for c in range(CB, NC):
        out += [("xT", c), ("lg", c - CB)]
    out += [("lg", NC - CB + i) for i in range(CB)]
    out += [("route", 0), ("qk", 0), ("V", 0), ("weights", 0), ("sh", (0, 0)), ("pos", 0), ("pos", 1)]
    out += [("att", (0, 0)), ("att", (0, 1)), ("hot", 0), ("att", (0, 2)), ("att", (0, 3)), ("oh", 0),
            ("proj", 1), ("hot", 1), ("mT", 0), ("sh", (0, 1)),
            ("att", (1, 0)), ("att", (1, 1)), ("oh", 1), ("hot", 2), ("att", (1, 2)), ("att", (1, 3)), ("oh", 2), ("hot", 3),
            ("mT", 1), ("qk", 1), ("sh", (0, 2)), ("oh", 3), ("disp", 0), ("slots", 0), ("wperm", 0)]
    PROJ_STEPS = (2, 4, 6, 7, 8, 9)
    for s in range(2, NA + 3):
        experts = []
        for g in (2 * (s - 3), 2 * (s - 3) + 1) if s >= 3 else ():
            experts.append([("xg", g), ("gu", g), ("aT", g), ("dn", g)] if g < NG else [])
        experts = experts or [[], []]
        fill = []
        if s in PROJ_STEPS:
            fill.append(("proj", 2 + PROJ_STEPS.index(s)))
        if s % 4 == 1 and s < NA:
            fill.append(("V", s // 4))
        if 6 < s < NA - 1 and s % 4 != 2:
            fill.append(("sh", ((s - 3) // 4, (s - 3) % 4)))
        if s in (NA - 1, NA):
            fill += [("sh", (B - 1, m)) for m in ((0, 1) if s == NA - 1 else (2,))]
        if s == NA + 1:
            fill += [("fsh", NC - CB + i) for i in range(CB)]
        if s >= 6 and s % 4 == 2:
            fill += [("fin", s - 6 + i) for i in range(CB)]
        if s < NA + 2:
            for q in range(4):
                out.append(("att", (s, q)))
                c = 4 * (s - 12) + q - 2
                if 0 <= c < NC:
                    out += [("comb", c)] + [("gather", c + CB)] * (c + CB < NC)
                if s == 3 and q == 1:
                    out.append(("qk", 2))
                out += experts[0][q:q + 1]
        if s >= 3 and s % 2 == 1 and s < NA + 2:
            out.append(("norm", (s - 3) // 2))
        if s < NA:
            out += fill[:1] + [("mT", s)]
            fill = fill[1:]
        while experts[1] or fill:
            out += experts[1][:1] + fill[:1]
            experts[1], fill = experts[1][1:], fill[1:]
        if s % 2 == 0 and 4 <= s and s // 2 + 1 < NU:
            out.append(("qk", s // 2 + 1))
        if s == 11:
            out += [("gather", i) for i in range(CB)]
        if s in (13, 14, 16):
            out += [("store", CB * {13: 0, 14: 1, 16: 2}[s] + i) for i in range(CB)]
    out += [("store", c) for c in range(12, NC)]
    return out


SCHED = schedule()
RING = {"wT": (1, "act"), "xT": (1, "act"), "lg": (1, "act"), "pos": (1, "dve"), "wperm": (1, "act"),
        "proj": (2, "dve"), "V": (2, "act"), "mT": (1, "act"), "xg": (1, "act"), "gu": (1, "dve"),
        "aT": (1, "act"), "dn": (1, "act"), "sh": (2, "dve"), "fsh": (1, "dve"), "fin": (1, "dve")}


EARLY_BANKS = 5


def ring_counts():
    fill, emptied, banks, before, count, last = {}, [], [], [], {"act": 0, "dve": 0}, {}
    early = True
    for stage in SCHED:
        early = early and stage[0] != "att"
        if stage[0] in RING:
            fill[stage] = len(emptied)
            k, engine = RING[stage[0]]
            for _ in range(k):
                n = len(emptied)
                count[engine] += 1
                emptied.append((engine, count[engine]))
                banks.append(n % (EARLY_BANKS if early else 2))
                before.append(last.get(banks[n]))
                last[banks[n]] = n
    return fill, emptied, banks, before


FILL, EMPTIED, BANKS, BEFORE = ring_counts()
LAST_EARLY = FILL[("pos", 1)]


def program(nc, x, wq, wk, wv, wo, gate_w, w_gate, w_up, w_down, sw_gate, sw_up, sw_down, const, out):
    xn_rows = nc.dram_tensor("xn_rows", (T, D), F32, kind="Internal").ap()
    y_rows = nc.dram_tensor("y_rows", (1 + E * CAP, D), F32, kind="Internal").ap()
    parts_d = nc.dram_tensor("parts_d", (2, 2, 3, DK, HB, S), BF16, kind="Internal").ap()

    with ExitStack() as ctx:
        def sb(name, shape, dt=F32):
            return ctx.enter_context(nc.sbuf_tensor(name, shape, dt))

        def bank(name):
            return ctx.enter_context(nc.psum_tensor(name, [P, 512], F32))

        def sem(name):
            return ctx.enter_context(nc.semaphore(name))

        cst = sb("cst", [P, C_END])
        cstb = sb("cstb", [P, C_END - C_TRI], BF16)
        identb = sb("identb", [P, P], BF16)
        onesb = sb("onesb", [P, P], BF16)
        onehat = sb("onehat", [P, 2, 32])
        graw = sb("graw", [E, D])
        wT = sb("wT", [P, 4, 2, D])
        gT = sb("gT", [P, 2, E])
        swg = sb("swg", [P, 2, IS])
        swu = sb("swu", [P, 2, IS])
        swd = sb("swd", [P, 3, D])
        acc = sb("acc", [P, NC, D])
        xnT = sb("xnT", [P, 2, T])
        st6 = sb("st6", [P, B, CB, 6])
        mv = sb("mv", [P, B, CB, 2])
        vareps = sb("vareps", [P, B, CB])
        std = sb("std", [P, B, CB])
        rstd = sb("rstd", [P, B, CB])
        newton = sb("newton", [P, B, CB])
        def carver(region):
            at = [0]

            def carve(n, dt=F32):
                lo = at[0]
                at[0] += n if dt == F32 else n // 2
                return region[:, lo:at[0]] if dt == F32 else region[:, lo:at[0]].bitcast(dt)
            return carve

        probs = sb("probs", [P, PT_W])
        att_mem = sb("att_mem", [P, CB * H * 32 + 2 * S + 3 * S])
        carve = carver(att_mem)
        vhat = carve(CB * H * 32).rearrange("p (c h w) -> p c h w", c=CB, h=H)
        aT = carve(2 * S).rearrange("p (k t) -> p k t", k=2)
        hT = carve(3 * S).rearrange("p (m t) -> p m t", m=3)
        carve = carver(att_mem)
        xn = carve(NC * D).rearrange("p (c d) -> p c d", c=NC)
        wgu_mem = sb("wgu_mem", [P, 2 * 2 * EG * 2 * I])
        carve = carver(wgu_mem)
        L = carve(NC * (E + 2)).rearrange("p (c e) -> p c e", c=NC)
        key = L[:, :, 0:E]
        Lrep = carve(NC * (E + 2)).rearrange("p (c e) -> p c e", c=NC)
        valid = Lrep[:, :, 0:E]
        mask = carve(NC * E, BF16).rearrange("p (c e) -> p c e", c=NC)
        cum = carve(NC * E, BF16).rearrange("p (c e) -> p c e", c=NC)
        ex = carve(NC * E).rearrange("p (c e) -> p c e", c=NC)
        pos1 = carve(NC * E, BF16).rearrange("p (c e) -> p c e", c=NC)
        carve = carver(wgu_mem)
        wraw = carve(8 * D).rearrange("p (w o d) -> p w o d", w=4, o=2)
        top8 = sb("top8", [P, NC, 8])
        negtop = sb("negtop", [P, NC])
        exsum = sb("exsum", [P, NC])
        rsum = sb("rsum", [P, NC])
        slot8 = sb("slot8", [P, NC, 8])
        slotu = sb("slotu", [P, NC, 8], U32)
        got = sb("got", [P, NG, NDV])
        tokf = sb("tokf", [P, NG])
        toku = sb("toku", [P, NG], U32)
        w3 = sb("w3", [P, NG, EG])
        wgot = sb("wgot", [P, NG])
        wslot = sb("wslot", [P, NG])
        exp_mem = sb("exp_mem", [P, 4 * D + 4 * P + 2 * D])
        carve = carver(exp_mem)
        xg = carve(4 * D).rearrange("p (a d) -> p a d", a=4)
        xgT = carve(4 * P).rearrange("p (a k t) -> p a k t", a=2, k=2)
        ys = carve(2 * D).rearrange("p (a d) -> p a d", a=2)
        carve = carver(exp_mem)
        disp = carve(NC * NG * NDV, BF16).rearrange("p (c g n) -> p c g n", c=NC, g=NG)
        wgu = wgu_mem[:, :].rearrange("p (a g e k i) -> p a g e k i", a=2, g=2, e=EG, k=2)
        wdn = sb("wdn", [P, 2, EG, 2, D])
        onehot = wdn[:, :, :, :, :].rearrange("p a e k d -> p (a e k d)").bitcast(BF16).rearrange(
            "p (n k e) -> p n k e", k=CAP, e=EG)
        th = sb("th", [P, I])
        ga = sb("ga", [P, I])
        hx = sb("hx", [P, I])
        hxT = sb("hxT", [IH, 2, P])
        zrow = sb("zrow", [1, D])
        tsh = sb("tsh", [P, S])
        gsh = sb("gsh", [P, S])
        rots = sb("rots", [P, 2, 2, S])
        rot1, rot2 = rots[:, 0, :, :], rots[:, 1, :, :]
        parts = sb("parts", [P, 2, 3, S], BF16)
        q6 = sb("q6", [P, 2, HB, S], BF16)
        k6 = sb("k6", [P, 2, HB, S], BF16)
        mx = sb("mx", [P, CB, 4])
        mres = sb("mres", [P, CB, 4])
        mp = sb("mp", [P, 2, CB, 3, 4], BF16)
        mrow = sb("mrow", [12, 2, S], BF16)
        recip = gsh
        wdn_flat = wdn[:, :, :, :, :].rearrange("p a e k d -> p (a e k d)")
        NGB = 4
        gb = [m[:, i * TOPK * D:(i + 1) * TOPK * D].rearrange("p (k d) -> p k d", k=TOPK)
              for m in (wdn_flat, wgu_mem) for i in range(NGB // 2)]
        ysum = wdn_flat[:, 2 * TOPK * D:(2 * TOPK + 1) * D]
        pmax = [bank(f"pmax{i}") for i in range(2)]
        psc = [bank(f"psc{i}") for i in range(2)]
        pO = bank("pO")
        pD = bank("pD")
        ring = [bank(f"ring{i}") for i in range(2)] + psc + [pO]

        id_in = sem("id_in"); c_in = sem("c_in"); w_in = sem("w_in"); sw_in = sem("sw_in")
        x_in = [sem(f"x_in{b}") for b in range(B)]
        xn_out = sem("xn_out")
        const_b = sem("const_b"); rsum_ready = sem("rsum_ready"); pool_set = sem("pool_set");
        var_ready = sem("var_ready"); std_ready = sem("std_ready")
        xn_ready = sem("xn_ready")
        ring_full = sem("ring_full"); act_emptied = sem("act_emptied"); dve_emptied = sem("dve_emptied")
        mask_ready = sem("mask_ready"); negtop_ready = sem("negtop_ready"); ex_ready = sem("ex_ready")
        cum_ready = sem("cum_ready"); onehot_ready = sem("onehot_ready"); onehot_used = sem("onehot_used")
        pos1_ready = sem("pos1_ready")
        weights_ready = sem("weights_ready"); got_ready = sem("got_ready")
        slots_ready = sem("slots_ready"); tok_ready = sem("tok_ready")
        xg_in = [sem(f"xg_in{i}") for i in range(4)]
        wgu_in = [sem(f"wgu_in{i}") for i in range(2)]
        wdn_in = [sem(f"wdn_in{i}") for i in range(2)]
        tanh_ready = sem("tanh_ready"); hx_ready = sem("hx_ready")
        y_out = [sem(f"y_out{i}") for i in range(2)]
        z_out = sem("z_out")
        tsh_ready = sem("tsh_ready")
        rot_ready = sem("rot_ready"); parts_ready = sem("parts_ready")
        parts_out = sem("parts_out")
        qk_in = [sem(f"qk_in{i}") for i in range(2)]
        max_full = sem("max_full"); max_emptied = sem("max_emptied"); mp_ready = sem("mp_ready")
        m_in = [sem(f"m_in{i}") for i in range(2)]
        sc_full = sem("sc_full"); exp_done = sem("exp_done")
        pv_done = sem("pv_done"); norm_done = sem("norm_done")
        gb_in = [sem(f"gb_in{i}") for i in range(NGB)]
        gb_used = sem("gb_used"); acc_done = sem("acc_done"); out_done = sem("out_done")
        dve_chain = sem("dve_chain"); pool_chain = sem("pool_chain")

        def emptied(eng, stage, k=None):
            n = FILL[stage] + (RING[stage[0]][0] - 1 if k is None else k)
            engine, count = EMPTIED[n]
            eng.wait_ge(act_emptied if engine == "act" else dve_emptied, count)

        def filled(eng, stage, k=0):
            n = FILL[stage] + k
            eng.wait_ge(ring_full, n + 1)
            return ring[BANKS[n]]

        order = {}
        for kind, arg in SCHED:
            order[(kind, arg)] = sum(1 for k2, _ in order if k2 == kind)

        ident = cst[:, C_ID:C_ID + P]
        tri = cstb[:, 0:P]
        mask_qk = cstb[:, P:2 * P]
        mask_kq = cstb[:, 2 * P:3 * P]
        ids = cstb[:, 3 * P:3 * P + 2 * NC].rearrange("p (c t) -> p c t", t=2)
        cosT = cst[:, C_COS:C_COS + S]
        sinT = cst[:, C_SIN:C_SIN + S]
        x_v = x.rearrange("b (c p) d -> b p c d", p=P)
        xn_v = xn_rows.rearrange("(b c p) d -> b p c d", p=P, c=CB)
        out_v = out.rearrange("b (c p) d -> b c p d", p=P)

        def acc_count(c, kind):
            n = 0
            for k2, a2 in SCHED:
                if k2 in ("fin", "fsh", "comb"):
                    n += 1
                    if k2 == kind and a2 == c:
                        return n

        def split(engine, link, i):
            link(engine.tensor_add(rot1[:, i, :], rot1[:, i, :], rot2[:, i, :]))
            link(engine.tensor_copy(parts[:, i, 0, :], rot1[:, i, :]))
            link(engine.tensor_tensor(rot1[:, i, :], rot1[:, i, :], parts[:, i, 0, :], ALU.subtract))
            link(engine.tensor_copy(parts[:, i, 1, :], rot1[:, i, :]))
            engine.tensor_tensor(parts[:, i, 2, :], rot1[:, i, :], parts[:, i, 1, :], ALU.subtract
                                 ).then_inc(parts_ready, 1)

        def split_count(a):
            return 2 * (a + 1)

        block = ctx.enter_context(nc.Block())

        @block.sync
        def _(sp):
            sp.dma_start(acc[:, 0:CB, :], x_v[0]).then_inc(x_in[0], 16)
            sp.dma_start(cst[:, 0:C_COS], const[:, 0:C_COS]).then_inc(id_in, 16)
            for i, w in enumerate((wq, wk, wv, wo)):
                sp.dma_start(wraw[:, i, :, :], w.rearrange("(o p) d -> p o d", p=P)).then_inc(w_in, 16)
            sp.dma_start(graw[:, :], gate_w).then_inc(w_in, 16)
            sp.dma_start(cst[:, C_COS:C_END], const[:, C_COS:C_END]).then_inc(c_in, 16)
            for b in range(1, B):
                sp.dma_start(acc[:, CB * b:CB * b + CB, :], x_v[b]).then_inc(x_in[b], 16)
            sp.dma_start(swg[:, :, :], sw_gate.rearrange("(p k) i -> p k i", k=2)).then_inc(sw_in, 16)
            sp.dma_start(swu[:, :, :], sw_up.rearrange("(p k) i -> p k i", k=2)).then_inc(sw_in, 16)
            for m, (m0, mw) in enumerate(SM):
                sp.dma_start(swd[0:mw, m, :], sw_down[m0:m0 + mw, :]).then_inc(sw_in, 16)

            def load_experts(G):
                buf = G % 2
                if G >= 2:
                    emptied(sp, ("gu", G - 2))
                elif G == 0:
                    sp.wait_ge(slots_ready, 1)
                    sp.wait_ge(onehot_ready, 4)
                for i, w in enumerate((w_gate, w_up)):
                    sp.dma_start(wgu[:, buf, i, :, :, :].rearrange("p e k i -> p e (k i)"),
                                 w[EG * G:EG * G + EG].rearrange("e (p k) i -> p e (k i)", k=2)
                                 ).then_inc(wgu_in[buf], 16)
                if G >= 2:
                    emptied(sp, ("dn", G - 2))
                else:
                    sp.wait_ge(onehot_used, 4)
                sp.dma_start(wdn[0:IH, buf, :, :, :].rearrange("p e k d -> p e (k d)"),
                             w_down[EG * G:EG * G + EG].rearrange("e (p k) d -> p e (k d)", k=2)
                             ).then_inc(wdn_in[buf], 16)

            for kind, a in SCHED:
                if kind == "lg" and a == NC - 1:
                    for b in range(B):
                        sp.wait_ge(xn_ready, CB * (b + 1))
                        sp.dma_start(xn_v[b], xn[:, CB * b:CB * b + CB, :]).then_inc(xn_out, 16)
                elif kind == "slots":
                    load_experts(0)
                    load_experts(1)
                    sp.wait_ge(pool_set, 1)
                    sp.dma_start(y_rows[0:1, :], zrow[:, :]).then_inc(z_out, 16)
                elif kind == "proj":
                    buf = a % 2
                    sp.wait_ge(parts_ready, split_count(a))
                    if a >= 2:
                        sp.wait_ge(qk_in[buf], 9 * 16 * (a // 2))
                    for i in range(2):
                        for t in range(3):
                            sp.dma_start(parts_d[buf, i, t].rearrange("d h n -> h d n"),
                                         parts[:, i, t, :]).then_inc(parts_out, 16)
                elif kind == "qk":
                    buf = a % 2
                    sp.wait_ge(parts_out, 6 * 16 * (a + 1))
                    if a >= 2:
                        sp.wait_ge(sc_full, NF * (2 * a - 2))
                    for t, src in enumerate((0, 0, 0, 1, 1, 2)):
                        sp.dma_start(q6[DK * t:DK * t + DK, buf, :, :], parts_d[buf, 0, src]
                                     ).then_inc(qk_in[buf], 16)
                    for t0, n in ((0, 3), (3, 2), (5, 1)):
                        sp.dma_start(k6[DK * t0:DK * (t0 + n), buf, :, :],
                                     parts_d[buf, 1, 0:n].rearrange("t d h n -> (t d) h n")
                                     ).then_inc(qk_in[buf], 16)
                elif kind == "dn":
                    emptied(sp, ("dn", a))
                    sp.dma_start(y_rows[1 + P * a:1 + P * a + P, :], ys[:, a % 2, :]).then_inc(y_out[a % 2], 16)
                    if a + 2 < NG:
                        load_experts(a + 2)
                elif kind == "store":
                    sp.wait_ge(acc_done, max(acc_count(a, "fin"), acc_count(a, "comb")))
                    sp.dma_start(out_v[a // CB, a % CB], acc[:, a, :]).then_inc(out_done, 16)
            sp.wait_ge(out_done, 16 * NC)

        @block.gpsimd
        def _(pool):
            links = [0]

            def link(ins):
                links[0] += 1
                ins.then_inc(pool_chain, 1)
                pool.wait_ge(pool_chain, links[0])

            nc.gpsimd.memset(zrow[:, :], 0.0).then_inc(pool_set, 1)
            nc.gpsimd.memset(onesb[:, :], 1.0).then_inc(pool_set, 1)
            link(nc.gpsimd.memset(onehat[:, :, :], 0.0))
            for i in range(2):
                nc.gpsimd.memset(onehat[:, i, DK * i:DK * i + DK], 1.0).then_inc(pool_set, 1)
            emptied(pool, ("wT", 3))
            nc.gpsimd.memset(L[:, :, E:E + 2], BIG).then_inc(pool_set, 1)
            pool.wait_ge(pool_set, 5)
            nc.gpsimd.memset(k6[KQ:P, :, :, :], 1.0).then_inc(pool_set, 1)
            pool.wait_ge(pool_set, 6)
            nc.gpsimd.memset(cum[:, 0, :], 0.0).then_inc(pool_set, 1)
            def gather_tokens(G):
                if G >= 4:
                    emptied(pool, ("xg", G - 4))
                pool.indirect_dma_start(out=xg[:, G % 4, :], out_offset=None, in_=xn_rows,
                                        in_offset=bass.IndirectOffsetOnAxis(ap=toku[:, G:G + 1], axis=0)
                                        ).then_inc(xg_in[G % 4], 16)

            for kind, a in SCHED:
                if kind == "proj":
                    for i in range(1 if a == 0 else 2):
                        pool.wait_ge(rot_ready, 2 * a + i + 1)
                        if a >= 1 and i == 0:
                            pool.wait_ge(parts_out, 6 * 16 * a)
                        split(nc.gpsimd, link, i)
                elif kind == "weights":
                    pool.wait_ge(rsum_ready, 1)
                    rb = rsum[:, :].rearrange("p (c o) -> p c o", o=1).broadcast_to([P, NC, E])
                    link(nc.gpsimd.tensor_tensor(ex[:, :, :], ex[:, :, :], rb, ALU.mult))
                    exg = ex[:, :, :].rearrange("p c (g e) -> p (c g) e", e=EG)
                    dg = disp[:, :, :, :].rearrange("p c g n -> p (c g) n")
                    part = [dg[:, :, 2 + EG * t:2 + EG * t + EG] for t in range(3)]
                    link(nc.gpsimd.tensor_copy(part[0], exg))
                    link(nc.gpsimd.tensor_tensor(exg, exg, part[0], ALU.subtract))
                    link(nc.gpsimd.tensor_copy(part[1], exg))
                    link(nc.gpsimd.tensor_tensor(part[2], exg, part[1], ALU.subtract))
                    idb = ids.rearrange("p c (o t) -> p c o t", o=1).broadcast_to([P, NC, NG, 2])
                    pool.wait_ge(const_b, 2)
                    nc.gpsimd.tensor_copy(disp[:, :, :, 0:2], idb).then_inc(weights_ready, 1)
                elif kind == "disp":
                    pool.wait_ge(tok_ready, 1)
                    pool.wait_ge(onehot_used, 4)
                    for G in range(4):
                        gather_tokens(G)
                elif kind == "xT" and a == NC - 1:
                    pool.wait_ge(xn_out, 16 * B)
                    emptied(pool, (kind, a))
                    nc.gpsimd.memset(vhat[:, :, :, :], 0.0).then_inc(pool_set, 1)
                elif kind == "xg" and a + 4 < NG:
                    gather_tokens(a + 4)
                elif kind == "gather":
                    if a == 0:
                        pool.wait_ge(slots_ready, 1)
                        pool.wait_ge(z_out, 16)
                        for i in range(2):
                            pool.wait_ge(y_out[i], 16 * (NG // 2))
                    if a >= NGB:
                        pool.wait_ge(gb_used, a - NGB + 1)
                    for k in range(TOPK):
                        pool.indirect_dma_start(out=gb[a % NGB][:, k, :], out_offset=None, in_=y_rows,
                                                in_offset=bass.IndirectOffsetOnAxis(
                                                    ap=slotu[:, a, k:k + 1], axis=0)
                                                ).then_inc(gb_in[a % NGB], 16)

        @block.scalar
        def _(act):
            act.wait_ge(id_in, 16)
            nc.scalar.activation(identb[:, :], ident, ACT.Copy).then_inc(const_b, 1)
            tanhs = 0
            for kind, a in SCHED:
                if kind == "wT":
                    r = filled(act, (kind, a))
                    if a < 4:
                        nc.scalar.activation(wT[:, a, :, :].rearrange("p k d -> p (k d)"), r[:, :],
                                             ACT.Copy).then_inc(act_emptied, 1)
                    else:
                        nc.scalar.activation(gT[:, :, :].rearrange("p k e -> p (k e)"), r[:, 0:2 * E],
                                             ACT.Copy).then_inc(act_emptied, 1)
                elif kind == "xT":
                    if a == 0 or a == CB:
                        bs = slice(0, 1) if a == 0 else slice(1, B)
                        act.wait_ge(var_ready, bs.stop)
                        nc.scalar.activation(std[:, bs, :], vareps[:, bs, :], ACT.Sqrt).then_inc(std_ready, 1)
                    r = filled(act, (kind, a))
                    nc.scalar.activation(xnT[:, :, P * a:P * a + P],
                                         r[:, 0:2 * P].rearrange("p (k t) -> p k t", k=2),
                                         ACT.Copy).then_inc(act_emptied, 1)
                elif kind == "lg":
                    r = filled(act, (kind, a))
                    nc.scalar.activation(L[:, a, 0:E], r[:, 0:E], ACT.Copy).then_inc(act_emptied, 1)
                elif kind == "route":
                    act.wait_ge(c_in, 16)
                    nc.scalar.activation(cstb[:, :], cst[:, C_TRI:C_END], ACT.Copy).then_inc(const_b, 1)
                    act.wait_ge(negtop_ready, 1)
                    emptied(act, ("lg", NC - 1))
                    for c in range(NC):
                        nc.scalar.activation(ex[:, c, :], L[:, c, 0:E], ACT.Exp, bias=negtop[:, c:c + 1],
                                             accum_out=exsum[:, c:c + 1]).then_inc(ex_ready, 1)
                elif kind == "V":
                    if a == 0:
                        act.wait_ge(pool_set, 8)
                    else:
                        act.wait_ge(pv_done, CB * 4 * a)
                    for i in range(2):
                        r = filled(act, (kind, a), i)[:, :].rearrange("p (c h2 e d) -> p c h2 e d", c=2, e=2, d=DK)
                        vv = vhat[:, 2 * i:2 * i + 2, :, :].rearrange("p c (h2 e) w -> p c h2 e w", e=2)
                        for cc in range(2):
                            for e in range(2):
                                last = nc.scalar.activation(vv[:, cc, :, e, DK * e:DK * e + DK],
                                                            r[:, cc, :, e, :], ACT.Copy)
                        last.then_inc(act_emptied, 1)
                elif kind == "mT":
                    if a >= 2:
                        act.wait_ge(m_in[a % 2], 48 * (a // 2))
                    r = filled(act, (kind, a))
                    nc.scalar.activation(mrow[:, a % 2, :], r[:, :].bitcast(BF16)[0:12, 0:S],
                                         ACT.Copy).then_inc(act_emptied, 1)
                    emptied(act, (kind, a))
                    for t in range(3):
                        act.dma_start(q6[KQ + t:KQ + t + 1, a // 2 % 2, a % 2::2, :],
                                      mrow[4 * t:4 * t + 4, a % 2, :]).then_inc(m_in[a % 2], 16)
                elif kind == "att" and 1 <= a[0] <= NA:
                    g = a[0] - 1
                    for i in EXP_Q[a[1]]:
                        kc, h0, n = SECOND[i]
                        act.wait_ge(sc_full, NF * g + i + 1)
                        if g >= 1:
                            act.wait_ge(pv_done, CB * (g - 1) + kc + 1)
                        w = S - P * kc
                        o = PT_OFF[kc] + h0 * w
                        nc.scalar.activation(probs[:, o:o + n * w], psc[(NF * g + i) % 2][:, 0:n * w],
                                             ACT.Exp, scale=DK ** -0.5).then_inc(exp_done, 1)
                elif kind == "xg":
                    r = filled(act, (kind, a))
                    if a >= 2:
                        emptied(act, ("gu", a - 2))
                    nc.scalar.activation(xgT[:, a % 2, :, :].rearrange("p k t -> p (k t)"), r[:, 0:2 * P],
                                         ACT.Copy).then_inc(act_emptied, 1)
                elif kind == "gu":
                    r = filled(act, (kind, a))
                    if a >= 1:
                        emptied(act, ("gu", a - 1))
                    nc.scalar.activation(th[:, :], r[:, 0:I], ACT.Tanh, scale=0.5).then_inc(tanh_ready, 1)
                elif kind == "aT":
                    r = filled(act, (kind, a))
                    nc.scalar.activation(hxT[:, :, :].rearrange("p k t -> p (k t)"), r[0:IH, 0:2 * P],
                                         ACT.Copy).then_inc(act_emptied, 1)
                elif kind == "wperm":
                    r = filled(act, (kind, a))
                    nc.scalar.activation(wslot[:, :], r[:, 0:NG], ACT.Copy).then_inc(act_emptied, 1)
                elif kind == "dn":
                    r = filled(act, (kind, a))
                    if a == 0:
                        emptied(act, ("wperm", 0))
                    if a >= 2:
                        act.wait_ge(y_out[a % 2], 16 * (a // 2))
                    nc.scalar.activation(ys[:, a % 2, :], r[:, 0:D], ACT.Copy,
                                         scale=wslot[:, a:a + 1]).then_inc(act_emptied, 1)
                elif kind == "sh":
                    m0, mw = SM[a[1]]
                    r = filled(act, (kind, a), 0)
                    tanhs += 1
                    if tanhs >= 2:
                        emptied(act, last_sh)
                    last_sh = (kind, a)
                    nc.scalar.activation(tsh[0:mw, :], r[0:mw, :], ACT.Tanh, scale=0.5).then_inc(tsh_ready, 1)

        @block.vector
        def _(dve):
            links = [0]

            def link(ins):
                links[0] += 1
                ins.then_inc(dve_chain, 1)
                dve.wait_ge(dve_chain, links[0])

            def variances(b):
                dve.wait_ge(x_in[b], 16)
                for c in range(CB):
                    last = nc.vector.bn_stats(st6[:, b, c, :], acc[:, CB * b + c, :])
                link(last)
                for c in range(CB):
                    last = nc.vector.bn_aggr(mv[:, b, c, :], st6[:, b, c, :])
                link(last)
                nc.vector.tensor_scalar(vareps[:, b, :], mv[:, b, :, 1], EPS, None, ALU.add).then_inc(var_ready, 1)

            shs = 0
            for kind, a in SCHED:
                if kind == "ln":
                    bs = slice(0, 1) if a == 0 else slice(1, B)
                    for b in range(bs.start, bs.stop):
                        variances(b)
                    dve.wait_ge(std_ready, 1 if a == 0 else 2)
                    link(nc.vector.reciprocal(rstd[:, bs, :], std[:, bs, :]))
                    link(nc.vector.tensor_tensor(newton[:, bs, :], vareps[:, bs, :], rstd[:, bs, :], ALU.mult))
                    link(nc.vector.tensor_tensor(newton[:, bs, :], newton[:, bs, :], rstd[:, bs, :], ALU.mult))
                    link(nc.vector.tensor_scalar(newton[:, bs, :], newton[:, bs, :], -0.5, 1.5, ALU.mult, ALU.add))
                    link(nc.vector.tensor_tensor(rstd[:, bs, :], rstd[:, bs, :], newton[:, bs, :], ALU.mult))
                    for c in range(CB * bs.start, CB * bs.stop):
                        nc.vector.tensor_scalar(xn[:, c, :], acc[:, c, :], mv[:, c // CB, c % CB, 0:1],
                                                rstd[:, c // CB, c % CB:c % CB + 1], ALU.subtract, ALU.mult
                                                ).then_inc(xn_ready, 1)
                elif kind == "route":
                    emptied(dve, ("lg", NC - 1))
                    dve.wait_ge(pool_set, 7)
                    for c in range(NC):
                        last = nc.vector.max(top8[:, c, :], L[:, c, :])
                    link(last)
                    nc.vector.tensor_scalar(negtop[:, :], top8[:, :, 2], -1.0, None, ALU.mult).then_inc(negtop_ready, 1)
                    for c in range(NC):
                        last = nc.vector.match_replace(Lrep[:, c, :], top8[:, c, :], L[:, c, :], -BIG)
                    link(last)
                    nc.vector.tensor_tensor(mask[:, :, :], L[:, :, 0:E], Lrep[:, :, 0:E], ALU.is_gt
                                            ).then_inc(mask_ready, 1)
                    dve.wait_ge(mask_ready, 1)
                    for c in range(1, NC):
                        nc.vector.tensor_tensor(cum[:, c, :], cum[:, c - 1, :], mask[:, c - 1, :], ALU.add
                                                ).then_inc(cum_ready, 1)
                        dve.wait_ge(cum_ready, c)
                elif kind == "pos":
                    if a == 0:
                        dve.wait_ge(ex_ready, NC)
                        dve.wait_ge(c_in, 16)
                    r = filled(dve, (kind, a))[:, :].rearrange("p (c e) -> p c e", e=E)
                    cs = slice(8 * a, 8 * a + 8)
                    base = cst[:, C_BASE:C_BASE + E].rearrange("p (o e) -> p o e", o=1).broadcast_to([P, 8, E])
                    link(nc.vector.scalar_tensor_tensor(valid[:, cs, :], r, float(CAP), mask[:, cs, :],
                                                        ALU.is_lt, ALU.mult))
                    nc.vector.tensor_tensor(key[:, cs, :], r, base, ALU.add)
                    nc.vector.scalar_tensor_tensor(pos1[:, cs, :], r, 1.0, valid[:, cs, :],
                                                   ALU.add, ALU.mult).then_inc(dve_emptied, 1)
                    emptied(dve, (kind, a))
                    dve.sem_inc(pos1_ready, 1)
                    link(nc.vector.tensor_tensor(key[:, cs, :], key[:, cs, :], valid[:, cs, :], ALU.mult))
                elif kind == "weights":
                    dve.wait_ge(ex_ready, NC)
                    nc.vector.reciprocal(rsum[:, :], exsum[:, :]).then_inc(rsum_ready, 1)
                elif kind == "hot":
                    if a >= 1:
                        dve.wait_ge(onehot_used, a)
                    src = pos1[:, 4 * a:4 * a + 4, :].rearrange("p c (g e) -> p (c g) e", e=EG)
                    for k in range(CAP):
                        last = nc.vector.tensor_scalar(onehot[:, :, k, :], src, float(k + 1), None, ALU.is_equal)
                    last.then_inc(onehot_ready, 1)
                elif kind == "disp":
                    dve.wait_ge(onehot_used, 4)
                    link(nc.vector.tensor_copy(got[:, :, :].rearrange("p g n -> p (g n)"), pD[:, 0:NG * NDV]))
                    link(nc.vector.scalar_tensor_tensor(tokf[:, :], got[:, :, 0], float(P), got[:, :, 1],
                                                        ALU.mult, ALU.add))
                    nc.vector.tensor_copy(toku[:, :], tokf[:, :]).then_inc(tok_ready, 1)
                    link(nc.vector.tensor_tensor(w3[:, :, :], got[:, :, 2:2 + EG], got[:, :, 2 + EG:2 + 2 * EG], ALU.add))
                    link(nc.vector.tensor_tensor(w3[:, :, :], w3[:, :, :], got[:, :, 2 + 2 * EG:NDV], ALU.add))
                    own = cst[:, C_OWN:C_OWN + EG].rearrange("p (o e) -> p o e", o=1).broadcast_to([P, NG, EG])
                    link(nc.vector.tensor_tensor(w3[:, :, :], w3[:, :, :], own, ALU.mult))
                    nc.vector.tensor_reduce(wgot[:, :], w3[:, :, :], AX.X, ALU.add).then_inc(tok_ready, 1)
                elif kind == "slots":
                    for c in range(NC):
                        last = nc.vector.max(slot8[:, c, :], key[:, c, :])
                    link(last)
                    nc.vector.tensor_copy(slotu[:, :, :], slot8[:, :, :]).then_inc(slots_ready, 1)
                elif kind == "proj":
                    if a == 0:
                        dve.wait_ge(c_in, 16)
                    for i in range(2):
                        if a >= 1 and i == 0:
                            dve.wait_ge(parts_ready, split_count(a - 1))
                        r = filled(dve, (kind, a), i)
                        nc.vector.tensor_tensor(rot1[:, i, :], r[:, :], cosT, ALU.mult)
                        nc.vector.stream_shuffle(rot2[:, i, :], r[:, :], [j ^ 1 for j in range(32)]
                                                 ).then_inc(dve_emptied, 1)
                        emptied(dve, (kind, a), i)
                        nc.vector.tensor_tensor(rot2[:, i, :], rot2[:, i, :], sinT, ALU.mult).then_inc(rot_ready, 1)
                    if a == 0:
                        dve.wait_ge(rot_ready, 2)
                        split(nc.vector, link, 1)
                elif kind == "att" and a[0] < NA:
                    g, q = a
                    for i in MAX_Q[q]:
                        qc, h0, n = FIRST[i]
                        w = P * (qc + 1)
                        dve.wait_ge(max_full, NF * g + i + 1)
                        r = pmax[(NF * g + i) % 2][:, 0:n * w].rearrange("p (h w) -> p h w", h=n)
                        nc.vector.tensor_reduce(mx[:, qc, h0:h0 + n], r, AX.X, ALU.max).then_inc(max_emptied, 1)
                    if q < 3:
                        continue
                    dve.wait_ge(max_emptied, NF * (g + 1))
                    if g >= 2:
                        emptied(dve, ("mT", g - 2))
                    m = mp[:, g % 2, :, :, :]
                    link(nc.vector.tensor_scalar(m[:, :, 0, :], mx[:, :, :], -1.0, None, ALU.mult))
                    link(nc.vector.scalar_tensor_tensor(mres[:, :, :], mx[:, :, :], -1.0, m[:, :, 0, :],
                                                        ALU.mult, ALU.subtract))
                    link(nc.vector.tensor_copy(m[:, :, 1, :], mres[:, :, :]))
                    nc.vector.tensor_tensor(m[:, :, 2, :], mres[:, :, :], m[:, :, 1, :],
                                            ALU.subtract).then_inc(mp_ready, 1)
                    dve.wait_ge(mp_ready, g + 1)
                elif kind == "gu":
                    r = filled(dve, (kind, a))
                    dve.wait_ge(tanh_ready, a + 1)
                    if a >= 1:
                        emptied(dve, ("aT", a - 1))
                    link(nc.vector.scalar_tensor_tensor(ga[:, :], th[:, :], 1.0, r[:, 0:I], ALU.add, ALU.mult))
                    nc.vector.scalar_tensor_tensor(hx[:, :], ga[:, :], 0.5, r[:, I:2 * I], ALU.mult, ALU.mult
                                                   ).then_inc(dve_emptied, 1)
                    emptied(dve, (kind, a))
                elif kind == "sh":
                    b, m = a
                    mw = SM[m][1]
                    shs += 1
                    dve.wait_ge(tsh_ready, shs)
                    r = filled(dve, (kind, a), 0)
                    nc.vector.scalar_tensor_tensor(gsh[0:mw, :], tsh[0:mw, :], 1.0, r[0:mw, :], ALU.add, ALU.mult
                                                   ).then_inc(dve_emptied, 1)
                    emptied(dve, (kind, a), 0)
                    if b >= 1 and m == 0:
                        emptied(dve, ("fin", CB * b - 1))
                    r = filled(dve, (kind, a), 1)
                    nc.vector.scalar_tensor_tensor(hT[0:mw, m, :], gsh[0:mw, :], 0.5, r[0:mw, :],
                                                   ALU.mult, ALU.mult).then_inc(dve_emptied, 1)
                    emptied(dve, (kind, a), 1)
                elif kind == "norm":
                    b, blk = a // 2, a % 2
                    dve.wait_ge(pv_done, CB * (2 * a + 2))
                    if b >= 1 and blk == 0:
                        emptied(dve, ("fin", CB * b - 1))
                    link(nc.vector.reciprocal(recip[:, :], pD[:, :]))
                    nc.vector.tensor_tensor(aT[:, blk, :], pO[:, :], recip[:, :], ALU.mult
                                            ).then_inc(norm_done, 1)
                    dve.wait_ge(norm_done, a + 1)
                elif kind in ("fin", "fsh"):
                    r = filled(dve, (kind, a))
                    dve.wait_ge(xn_ready, NC)
                    link(nc.vector.tensor_tensor(acc[:, a, :], acc[:, a, :], r[:, 0:D], ALU.add))
                    dve.sem_inc(dve_emptied, 1)
                    dve.sem_inc(acc_done, 1)
                elif kind == "comb":
                    dve.wait_ge(gb_in[a % NGB], TOPK * 16 * (a // NGB + 1))
                    nc.vector.tensor_reduce(ysum[:, :], gb[a % NGB].rearrange("p k d -> p d k"), AX.X,
                                            ALU.add).then_inc(gb_used, 1)
                    dve.wait_ge(gb_used, a + 1)
                    link(nc.vector.tensor_tensor(acc[:, a, :], acc[:, a, :], ysum[:, :], ALU.add))
                    dve.sem_inc(acc_done, 1)

        @block.tensor
        def _(pe):
            def wait_emptied(n):
                engine, count = EMPTIED[n]
                pe.wait_ge(act_emptied if engine == "act" else dve_emptied, count)

            def claim(stage, k=0):
                n = FILL[stage] + k
                if BEFORE[n] is not None:
                    wait_emptied(BEFORE[n])
                return ring[BANKS[n]]

            def scores_for_max(g, i):
                u, hg = g // 2, g % 2
                qc, h0, n = FIRST[i]
                f = NF * g + i
                if f >= 2:
                    pe.wait_ge(max_emptied, f - 1)
                w = P * (qc + 1)
                for j in range(n):
                    h = 2 * (h0 + j) + hg
                    o = pmax[f % 2][:, w * j:w * j + w]
                    nc.tensor.matmul(o, q6[0:KQ, u % 2, h, P * qc:P * qc + P], k6[0:KQ, u % 2, h, 0:w],
                                     start=True, stop=False)
                    last = nc.tensor.matmul(o[:, w - P:w], identb[:, :], mask_qk, start=False, stop=True)
                last.then_inc(max_full, 1)

            def scores_for_exp(g, i):
                u, hg = g // 2, g % 2
                kc, h0, n = SECOND[i]
                f = NF * g + i
                if f >= 2:
                    pe.wait_ge(exp_done, f - 1)
                w = S - P * kc
                for j in range(n):
                    h = 2 * (h0 + j) + hg
                    o = psc[f % 2][:, w * j:w * j + w]
                    nc.tensor.matmul(o, k6[0:KM, u % 2, h, P * kc:P * kc + P], q6[0:KM, u % 2, h, P * kc:S],
                                     start=True, stop=False)
                    last = nc.tensor.matmul(o[:, 0:P], identb[:, :], mask_kq, start=False, stop=True)
                last.then_inc(sc_full, 1)

            def values_begin(g):
                u = g // 2
                emptied(pe, ("V", u // 2))
                if g % 2 == 0 and u >= 1:
                    pe.wait_ge(norm_done, u)

            def values(g, kc, which):
                u, hg = g // 2, g % 2
                w = S - P * kc
                for n in which:
                    j = n % 4
                    if n == 0:
                        pe.wait_ge(exp_done, NF * g + max(i for i in range(NF) if SECOND[i][0] == kc) + 1)
                    v = vhat[:, kc, HB * (u % 2) + 2 * j + hg, :] if n < 4 else onehat[:, hg, :]
                    dst = pO if n < 4 else pD
                    o = PT_OFF[kc] + w * j
                    last = nc.tensor.matmul(dst[32 * j:32 * j + 32, P * kc:S], v, probs[:, o:o + w],
                                            start=(hg == 0 and kc == 0), stop=(hg == 1 and kc == CB - 1),
                                            skip_group_check=True)
                    if n == 7:
                        last.then_inc(pv_done, 1)

            pe.wait_ge(id_in, 16)
            pe.wait_ge(w_in, 5 * 16)
            for kind, a in SCHED:
                if kind == "wT":
                    r = claim((kind, a))
                    for k in range(2):
                        if a == 4:
                            last = nc.tensor.transpose(r[:, E * k:E * k + E], graw[:, k::2], ident[0:E, 0:E])
                            continue
                        for o in range(2):
                            src = wraw[:, a, o, k::2] if a < 3 else wraw[:, a, o, P * k:P * k + P]
                            last = nc.tensor.transpose(r[:, D * k + P * o:D * k + P * o + P], src, ident)
                    last.then_inc(ring_full, 1)
                elif kind == "xT":
                    r = claim((kind, a))
                    pe.wait_ge(xn_ready, a + 1)
                    for k in range(2):
                        last = nc.tensor.transpose(r[:, P * k:P * k + P], xn[:, a, k::2], ident)
                    last.then_inc(ring_full, 1)
                elif kind == "lg":
                    r = claim((kind, a))
                    emptied(pe, ("xT", a))
                    for k in range(2):
                        last = nc.tensor.matmul(r[:, 0:E], xnT[:, k, P * a:P * a + P], gT[:, k, :],
                                                start=(k == 0), stop=(k == 1))
                    last.then_inc(ring_full, 1)
                elif kind == "pos":
                    r = claim((kind, a))
                    pe.wait_ge(const_b, 2)
                    pe.wait_ge(pool_set, 2)
                    pe.wait_ge(cum_ready, NC - 1)
                    for c in range(8 * a, 8 * a + 8):
                        o = r[:, E * (c % 8):E * (c % 8) + E]
                        nc.tensor.matmul(o, tri, mask[:, c, :], start=True, stop=False)
                        last = nc.tensor.matmul(o, onesb[:, :], cum[:, c, :], start=False, stop=True)
                    last.then_inc(ring_full, 1)
                elif kind == "oh":
                    pe.wait_ge(weights_ready, 1)
                    pe.wait_ge(onehot_ready, a + 1)
                    for c in range(4 * a, 4 * a + 4):
                        for G in range(NG):
                            last = nc.tensor.matmul(
                                pD[:, NDV * G:NDV * G + NDV],
                                onehot[:, (c % 4) * NG + G, :, :].rearrange("p k e -> p (k e)"), disp[:, c, G, :],
                                start=(c == 0 and G == 0), stop=(c == NC - 1), skip_group_check=True)
                    last.then_inc(onehot_used, 1)
                elif kind == "wperm":
                    r = claim((kind, a))
                    pe.wait_ge(tok_ready, 2)
                    nc.tensor.matmul(r[:, 0:NG], cst[:, C_PERM:C_PERM + P], wgot[:, :], start=True, stop=True
                                     ).then_inc(ring_full, 1)
                elif kind == "proj":
                    b, blk = a // 2, a % 2
                    emptied(pe, ("xT", CB * (b + 1) - 1))
                    for i in range(2):
                        r = claim((kind, a), i)
                        for k in range(2):
                            last = nc.tensor.matmul(r[:, :], wT[:, i, k, P * blk:P * blk + P],
                                                    xnT[:, k, S * b:S * b + S], start=(k == 0), stop=(k == 1))
                        last.then_inc(ring_full, 1)
                elif kind == "V":
                    for i in range(2):
                        r = claim((kind, a), i)
                        for cc in range(2):
                            c = CB * a + 2 * i + cc
                            for k in range(2):
                                last = nc.tensor.matmul(r[:, D * cc:D * cc + D], xnT[:, k, P * c:P * c + P],
                                                        wT[:, 2, k, :], start=(k == 0), stop=(k == 1))
                        last.then_inc(ring_full, 1)
                elif kind == "sh":
                    b, m = a
                    m0, mw = SM[m]
                    pe.wait_ge(sw_in, 5 * 16)
                    for i, w in enumerate((swg, swu)):
                        r = claim((kind, a), i)
                        for k in range(2):
                            last = nc.tensor.matmul(r[0:mw, :], w[:, k, m0:m0 + mw], xnT[:, k, S * b:S * b + S],
                                                    start=(k == 0), stop=(k == 1))
                        last.then_inc(ring_full, 1)
                elif kind == "att":
                    g, q = a
                    if q == 0 and g < NA:
                        pe.wait_ge(qk_in[g // 2 % 2], 9 * 16 * (g // 4 + 1))
                    if q == 1 and 1 <= g <= NA:
                        pe.wait_ge(m_in[(g - 1) % 2], 48 * ((g - 1) // 2 + 1))
                        if g == 1:
                            pe.wait_ge(pool_set, 6)
                            for n in range(EARLY_BANKS):
                                wait_emptied(LAST_EARLY - n)
                    if q == 0 and g >= 2:
                        values_begin(g - 2)
                    for i in range(4):
                        if i < len(MAX_Q[q]) and g < NA:
                            scores_for_max(g, MAX_Q[q][i])
                        if g >= 2:
                            values(g - 2, q, (2 * i, 2 * i + 1))
                        if i < len(EXP_Q[q]) and 1 <= g <= NA:
                            scores_for_exp(g - 1, EXP_Q[q][i])
                elif kind == "mT":
                    r = claim((kind, a))
                    pe.wait_ge(mp_ready, a + 1)
                    for qc in range(CB):
                        last = nc.tensor.transpose(r[:, :].bitcast(BF16)[0:12, P * qc:P * qc + P],
                                                   mp[:, a % 2, qc, :, :].rearrange("p t h -> p (t h)"), identb[:, :])
                    last.then_inc(ring_full, 1)
                elif kind == "xg":
                    r = claim((kind, a))
                    pe.wait_ge(xg_in[a % 4], 16 * (a // 4 + 1))
                    for k in range(2):
                        last = nc.tensor.transpose(r[:, P * k:P * k + P], xg[:, a % 4, k::2], ident)
                    last.then_inc(ring_full, 1)
                elif kind == "gu":
                    r = claim((kind, a))
                    pe.wait_ge(wgu_in[a % 2], 32 * (a // 2 + 1))
                    emptied(pe, ("xg", a))
                    for k in range(2):
                        for j in range(EG):
                            last = nc.tensor.matmul(r[32 * j:32 * j + 32, 0:2 * I],
                                                    xgT[:, a % 2, k, j::EG],
                                                    wgu[:, a % 2, :, j, k, :], start=(k == 0), stop=(k == 1))
                    last.then_inc(ring_full, 1)
                elif kind == "aT":
                    r = claim((kind, a))
                    emptied(pe, ("gu", a))
                    if a >= 1:
                        emptied(pe, ("dn", a - 1))
                    for k in range(2):
                        last = nc.tensor.transpose(r[0:IH, P * k:P * k + P], hx[:, k::2], ident)
                    last.then_inc(ring_full, 1)
                elif kind == "dn":
                    r = claim((kind, a))
                    pe.wait_ge(wdn_in[a % 2], 16 * (a // 2 + 1))
                    emptied(pe, ("aT", a))
                    for k in range(2):
                        for j in range(EG):
                            last = nc.tensor.matmul(r[32 * j:32 * j + 32, 0:D], hxT[:, k, CAP * j:CAP * j + CAP],
                                                    wdn[0:IH, a % 2, j, k, :], start=(k == 0), stop=(k == 1))
                    last.then_inc(ring_full, 1)
                elif kind in ("fin", "fsh"):
                    b, cq = a // CB, a % CB
                    r = claim((kind, a))
                    products = []
                    if kind == "fin":
                        pe.wait_ge(norm_done, 2 * b + 2)
                        products += [(aT[:, blk, P * cq:P * cq + P], wT[:, 3, blk, :]) for blk in range(2)]
                    if kind == "fsh" or b < B - 1:
                        emptied(pe, ("sh", (b, 2)), 1)
                        products += [(hT[0:mw, m, P * cq:P * cq + P], swd[0:mw, m, :]) for m, (_, mw) in enumerate(SM)]
                    for i, (lhsT, rhs) in enumerate(products):
                        last = nc.tensor.matmul(r[:, 0:D], lhsT, rhs, start=(i == 0), stop=(i == len(products) - 1))
                    last.then_inc(ring_full, 1)


def constants(np):
    f = np.float32
    c = np.zeros((P, C_END), f)
    c[:, C_ID:C_ID + P] = np.eye(P, dtype=f)
    inv = f(10000.0) ** (f(-2.0) * np.arange(DK // 2, dtype=f) / f(DK))
    ang = (np.arange(S, dtype=f)[:, None] * inv[None, :].astype(f)).astype(f)
    row = (np.arange(P) % DK) // 2
    sign = np.where(np.arange(P) % 2 == 0, f(-1), f(1))
    c[:, C_COS:C_COS + S] = np.cos(ang).T[row]
    c[:, C_SIN:C_SIN + S] = np.sin(ang).T[row] * sign[:, None]
    c[:, C_BASE:C_BASE + E] = (CAP * np.arange(E) + 1)[None, :]
    p = np.arange(P)
    c[:, C_OWN:C_OWN + EG] = p[:, None] % EG == np.arange(EG)[None, :]
    c[p, C_PERM + p % EG * CAP + p // EG] = 1
    c[:, C_TRI:C_TRI + P] = p[:, None] < p[None, :]
    c[:, C_M1:C_M1 + P] = np.where(p[None, :] > p[:, None], f(-1e30), f(0))
    c[:, C_M2:C_M2 + P] = np.where(p[:, None] > p[None, :], f(-1e30), f(0))
    c[:, C_IDS:C_IDS + 2 * NC:2] = np.arange(NC)[None, :]
    c[:, C_IDS + 1:C_IDS + 2 * NC:2] = p[:, None]
    return c


_INS = ["L0_attn_x", "L0_attn_wq", "L0_attn_wk", "L0_attn_wv", "L0_attn_wo", "L0_ffn_gate_w", "L0_ffn_w_gate",
        "L0_ffn_w_up", "L0_ffn_w_down", "L0_ffn_sw_gate", "L0_ffn_sw_up", "L0_ffn_sw_down"]


def kernel(**inputs):
    import numpy as _np
    import concourse.bacc as _bacc
    from concourse.bass_utils import run_bass_kernel_spmd as _run

    nc = _bacc.Bacc("TRN2", target_bir_lowering=False, num_devices=1)
    arrays, args = {}, []
    for name in _INS + ["const"]:
        a = constants(_np) if name == "const" else _np.ascontiguousarray(inputs[name])
        arrays[f"in_{name}"] = a
        args.append(nc.dram_tensor(f"in_{name}", a.shape, F32, kind="ExternalInput").ap())
    out = nc.dram_tensor("out0", (B, S, D), F32, kind="ExternalOutput").ap()
    program(nc, *args, out)
    r = _run(nc, [arrays], core_ids=[0])
    return r.results[0]["out0"]
```

```python
from contextlib import ExitStack

import concourse.bass as bass
from concourse import mybir

ALU = mybir.AluOpType
ACT = mybir.ActivationFunctionType
AX = mybir.AxisListType
F32 = mybir.dt.float32
BF16 = mybir.dt.bfloat16
U32 = mybir.dt.uint32

P = 128
B, S, D = 4, 512, 256
T = B * S
NC = T // P
CB = S // P
H, DK = 16, 16
HB = P // DK
E, TOPK, CAP, I = 64, 6, 32, 176
IH = I // 2
IS = 2 * I
EG = P // CAP
NG = E // EG
NU = B * 2
NA = 2 * NU
NT = 6
KQ = NT * DK
KM = KQ + 3
EPS = 1e-5
BIG = 3.0e38
SM = [(0, 128), (128, 128), (256, 96)]
NDV = 2 + 3 * EG

C_ID, C_COS, C_SIN, C_BASE, C_OWN, C_HALF, C_PERM, C_TRI, C_M1, C_M2, C_IDS, C_END = (
    0, 128, 640, 1152, 1216, 1220, 1222, 1350, 1478, 1606, 1734, 1766)


def score_fills():
    first = [(qc, h, n) for qc, n in ((0, 4), (1, 2), (2, 1), (3, 1)) for h in range(0, 4, n)]
    second = [(kc, h, n) for kc, n in ((0, 1), (1, 1), (2, 2), (3, 4)) for h in range(0, 4, n)]
    return first, second


FIRST, SECOND = score_fills()
NF = len(FIRST)
PT_OFF = [0, 4 * 512, 4 * (512 + 384), 4 * (512 + 384 + 256)]
PT_W = 4 * (512 + 384 + 256 + 128)


MAX_E = [0, 0, 2, 4, 5, 6, 8, 9, 10, 12, 13]
EXP_E = [4, 5, 6, 8, 8, 9, 11, 12, 14, 15, 15]
VAL_E = [0, 2, 3, 3, 4, 5, 6, 7, 8, 9, 10, 11, 12, 14, 15, 15]


def within(pieces, e):
    return [i for i, piece in enumerate(pieces) if piece == e]


TAKE_AT = [
    (3, 3), (4, 19), (7, 2), (9, 3), (11, 4), (13, 2), (15, 4), (16, 16),
]
NORM_AT = [
    [(3, 15), (3, 17), (4, 11), (4, 15)], [(5, 15), (6, 2), (6, 6), (6, 15)],
    [(7, 15), (7, 19), (8, 3), (8, 5)], [(9, 15), (9, 18), (10, 5), (10, 13)],
    [(11, 15), (11, 19), (12, 7), (12, 15)], [(13, 15), (13, 19), (14, 7), (14, 10)],
    [(15, 14), (15, 18), (16, 3), (16, 14)],
]
START = [
    ('ln', 0), ('wT', 0), ('wT', 1), ('wT', 2), ('wT', 3), ('wT', 4), ('xT', 2), ('ln', 1), ('xT', 0),
    ('xT', 1), ('xT', 3), ('proj', (0, 0)), ('proj', (0, 1)), ('ln', 2), ('xT', 4), ('lg', 0), ('xT', 5),
    ('lg', 3), ('lg', 1), ('xT', 7), ('xT', 6), ('lg', 2), ('ln', 3), ('lg', 4), ('xT', 8), ('xT', 9),
    ('lg', 5), ('xT', 10), ('lg', 6), ('xT', 11), ('lg', 7), ('xT', 12), ('lg', 8), ('xT', 13), ('lg', 9),
    ('xT', 14), ('lg', 10), ('xT', 15), ('lg', 11), ('lg', 12), ('lg', 13), ('lg', 14), ('lg', 15),
    ('route', 0), ('qk', 0), ('V', (0, 0)), ('V', (0, 1)), ('weights', 0), ('sh', (0, 0, 0)),
    ('sh', (0, 0, 1)), ('pos', 0), ('pos', 1),
]
GATHER_AT = [
    (10, 19), (10, 19), (10, 19), (11, 7),
]
QK_AT = [
    (1, 18), (3, 2), (5, 2), (7, 0), (9, 0), (11, 3), (13, 6),
]
COMB_AT = [
    (12, 11), (12, 15), (13, 8), (13, 12), (13, 16), (13, 19), (14, 15), (14, 15), (14, 19), (15, 4),
    (15, 7), (15, 11), (16, 1), (16, 9), (16, 10), (16, 14),
]
EXPERTS_AT = [
    [(3, 1), (3, 4), (3, 5), (3, 11)], [(3, 17), (3, 19), (4, 3), (4, 4)],
    [(4, 2), (4, 6), (4, 11), (4, 15)], [(4, 15), (4, 15), (4, 18), (4, 19)],
    [(5, 4), (5, 8), (5, 13), (5, 17)], [(5, 15), (5, 17), (5, 18), (6, 2)],
    [(6, 3), (6, 7), (6, 11), (6, 15)], [(6, 11), (6, 15), (6, 17), (6, 18)],
    [(7, 4), (7, 7), (7, 11), (7, 12)], [(7, 15), (7, 17), (7, 18), (7, 19)],
    [(8, 3), (8, 7), (8, 11), (8, 16)], [(8, 15), (8, 17), (8, 18), (8, 19)],
    [(8, 14), (9, 3), (9, 12), (9, 16)], [(9, 15), (9, 17), (9, 19), (10, 0)],
    [(10, 3), (10, 7), (10, 11), (10, 15)], [(10, 15), (10, 19), (11, 3), (11, 4)],
]
ONEHOT_AT = [
    (0, 7), (0, 15), (1, 7), (1, 15),
]
ONEHOT_USE_AT = [
    (0, 16), (1, 6), (1, 10), (1, 18),
]
V_AT = [
    (5, 13), (5, 19), (9, 16), (9, 17), (13, 17), (13, 18),
]
SHARED_AT = [
    (0, 19), (0, 19), (1, 17), (1, 17), (7, 17), (7, 17), (8, 17), (9, 1), (9, 19), (10, 2), (11, 16),
    (12, 1), (12, 17), (12, 17), (13, 15), (13, 15), (15, 7), (15, 13), (15, 15), (16, 1), (16, 19),
    (17, 0),
]
PROJ_AT = [
    (0, 15), (0, 17), (2, 6), (2, 11), (4, 13), (4, 15), (6, 15), (6, 16), (7, 16), (7, 17), (8, 16),
    (8, 17), (9, 13), (9, 16),
]
FIN_AT = [
    (6, 17), (6, 19), (6, 19), (7, 1), (10, 16), (10, 16), (10, 19), (11, 0), (14, 18), (14, 18), (14, 19),
    (14, 19),
]


def schedule():
    out = list(START)
    side = {}

    def put(kind, positions, args=None):
        for arg, at in zip(args or range(len(positions)), positions):
            side.setdefault(at, []).append((kind, arg))

    put("take", TAKE_AT)
    put("gather", GATHER_AT)
    put("qk", QK_AT, range(1, NU))
    for u, positions in enumerate(NORM_AT):
        put("norm", positions, [(u, q) for q in range(CB)])
    put("comb", COMB_AT)
    for n, positions in enumerate(EXPERTS_AT):
        for kind, at in zip(("xg", "gu", "aT", "dn"), positions):
            put(kind, [at], [n])
    put("oh", ONEHOT_USE_AT)
    put("V", V_AT, [(b, i) for b in range(1, B) for i in range(2)])
    put("proj", PROJ_AT, [(u, i) for u in range(1, NU) for i in range(2)])
    put("hot", ONEHOT_AT)
    put("sh", SHARED_AT, [(b, m, i) for b in range(B) for m in range(3) for i in range(2)][2:])
    put("fin", FIN_AT)
    for s in range(NA + 2):
        for e in range(16):
            out.append(("att", (s, e)))
            if s == NA + 1 and e % 4 == 3:
                out += [("norm", (NU - 1, e // 4)), ("fsh", NC - CB + e // 4), ("fin", NC - CB + e // 4)]
            out += side.pop((s, e), [])
        for place in range(16, 20):
            out += side.pop((s, place), [])
            if place == 16 and s < NA:
                out.append(("mT", s))
        if s == 1:
            out += [("disp", 0), ("slots", 0), ("wperm", 0)]
        if s == NA:
            out += [("store", i) for i in range(NC - CB)]
    assert not side, side
    out += [("store", c) for c in range(NC - CB, NC)]
    full = []
    for kind, a in out:
        full.append((kind, a))
        if kind == "comb" and a + CB < NC:
            full.append(("gather", a + CB))
    return full


SCHED = schedule()
RING = {"wT": (1, "act"), "xT": (1, "act"), "lg": (1, "act"), "pos": (1, "dve"), "wperm": (1, "act"),
        "proj": (1, "dve"), "V": (1, "act"), "mT": (1, "act"), "xg": (1, "act"), "gu": (1, "dve"),
        "aT": (1, "act"), "dn": (1, "act"), "sh": (1, "dve"), "fsh": (1, "dve"), "fin": (1, "dve")}


EARLY_BANKS = 5


def ring_counts():
    fill, emptied, banks, before, count, last = {}, [], [], [], {"act": 0, "dve": 0}, {}
    early = True
    for stage in SCHED:
        early = early and stage[0] != "att"
        if stage[0] in RING:
            fill[stage] = len(emptied)
            k, engine = RING[stage[0]]
            for _ in range(k):
                n = len(emptied)
                count[engine] += 1
                emptied.append((engine, count[engine]))
                banks.append(n % (EARLY_BANKS if early else 2))
                before.append(last.get(banks[n]))
                last[banks[n]] = n
    return fill, emptied, banks, before


FILL, EMPTIED, BANKS, BEFORE = ring_counts()
LAST_EARLY = max(FILL[stage] for stage in START if stage[0] in RING)


def program(nc, x, wq, wk, wv, wo, gate_w, w_gate, w_up, w_down, sw_gate, sw_up, sw_down, const, out):
    xn_rows = nc.dram_tensor("xn_rows", (T, D), F32, kind="Internal").ap()
    y_rows = nc.dram_tensor("y_rows", (1 + E * CAP, D), F32, kind="Internal").ap()
    parts_d = nc.dram_tensor("parts_d", (2, 2, 3, DK, HB, S), BF16, kind="Internal").ap()

    with ExitStack() as ctx:
        def sb(name, shape, dt=F32):
            return ctx.enter_context(nc.sbuf_tensor(name, shape, dt))

        def bank(name):
            return ctx.enter_context(nc.psum_tensor(name, [P, 512], F32))

        def sem(name):
            return ctx.enter_context(nc.semaphore(name))

        cst = sb("cst", [P, C_END])
        cstb = sb("cstb", [P, C_END - C_TRI], BF16)
        identb = sb("identb", [P, P], BF16)
        onesb = sb("onesb", [P, P], BF16)
        graw = sb("graw", [E, D])
        wT = sb("wT", [P, 4, 2, D])
        gT = sb("gT", [P, 2, E])
        swg = sb("swg", [P, 2, IS])
        swu = sb("swu", [P, 2, IS])
        swd = sb("swd", [P, 3, D])
        acc = sb("acc", [P, NC, D])
        xnT = sb("xnT", [P, 2, T])
        st6 = sb("st6", [P, B, CB, 6])
        mv = sb("mv", [P, B, CB, 2])
        vareps = sb("vareps", [P, B, CB])
        std = sb("std", [P, B, CB])
        rstd = sb("rstd", [P, B, CB])
        newton = sb("newton", [P, B, CB])
        def carver(region):
            at = [0]

            def carve(n, dt=F32):
                lo = at[0]
                at[0] += n if dt == F32 else n // 2
                return region[:, lo:at[0]] if dt == F32 else region[:, lo:at[0]].bitcast(dt)
            return carve

        probs = sb("probs", [P, PT_W])
        att_mem = sb("att_mem", [P, CB * H * 32 + 2 * S + 3 * S])
        carve = carver(att_mem)
        vhat = carve(CB * H * 32).rearrange("p (c h w) -> p c h w", c=CB, h=H)
        aT = carve(2 * S).rearrange("p (k t) -> p k t", k=2)
        hT = carve(3 * S).rearrange("p (m t) -> p m t", m=3)
        carve = carver(att_mem)
        xn = carve(NC * D).rearrange("p (c d) -> p c d", c=NC)
        wgu_mem = sb("wgu_mem", [P, 2 * 2 * EG * 2 * I])
        carve = carver(wgu_mem)
        L = carve(NC * (E + 2)).rearrange("p (c e) -> p c e", c=NC)
        key = L[:, :, 0:E]
        Lrep = carve(NC * (E + 2)).rearrange("p (c e) -> p c e", c=NC)
        valid = Lrep[:, :, 0:E]
        mask = carve(NC * E, BF16).rearrange("p (c e) -> p c e", c=NC)
        cum = carve(NC * E, BF16).rearrange("p (c e) -> p c e", c=NC)
        ex = carve(NC * E).rearrange("p (c e) -> p c e", c=NC)
        pos1 = carve(NC * E, BF16).rearrange("p (c e) -> p c e", c=NC)
        carve = carver(wgu_mem)
        wraw = carve(8 * D).rearrange("p (w o d) -> p w o d", w=4, o=2)
        top8 = sb("top8", [P, NC, 8])
        negtop = sb("negtop", [P, NC])
        exsum = sb("exsum", [P, NC])
        rsum = sb("rsum", [P, NC])
        slot8 = sb("slot8", [P, NC, 8])
        slotu = sb("slotu", [P, NC, 8], U32)
        got = sb("got", [P, NG, NDV])
        tokf = sb("tokf", [P, NG])
        toku = sb("toku", [P, NG], U32)
        w3 = sb("w3", [P, NG, EG])
        wgot = sb("wgot", [P, NG])
        wslot = sb("wslot", [P, NG])
        exp_mem = sb("exp_mem", [P, 4 * D + 4 * P + 2 * D])
        carve = carver(exp_mem)
        xg = carve(4 * D).rearrange("p (a d) -> p a d", a=4)
        xgT = carve(4 * P).rearrange("p (a k t) -> p a k t", a=2, k=2)
        ys = carve(2 * D).rearrange("p (a d) -> p a d", a=2)
        carve = carver(exp_mem)
        disp = carve(NC * NG * NDV, BF16).rearrange("p (c g n) -> p c g n", c=NC, g=NG)
        wgu = wgu_mem[:, :].rearrange("p (a g e k i) -> p a g e k i", a=2, g=2, e=EG, k=2)
        wdn = sb("wdn", [P, 2, EG, 2, D])
        onehot = wdn[:, :, :, :, :].rearrange("p a e k d -> p (a e k d)").bitcast(BF16).rearrange(
            "p (n k e) -> p n k e", k=CAP, e=EG)
        th = sb("th", [P, I])
        ga = sb("ga", [P, I])
        hx = sb("hx", [P, I])
        hxT = sb("hxT", [IH, 2, P])
        zrow = sb("zrow", [1, D])
        tsh = sb("tsh", [P, S])
        gsh = sb("gsh", [P, S])
        rots = sb("rots", [P, 2, 2, S])
        rot1, rot2 = rots[:, 0, :, :], rots[:, 1, :, :]
        parts = sb("parts", [P, 2, 3, S], BF16)
        q6 = sb("q6", [P, 2, HB, S], BF16)
        k6 = sb("k6", [P, 2, HB, S], BF16)
        mx = sb("mx", [P, CB, 4])
        mres = sb("mres", [P, CB, 4])
        mp = sb("mp", [P, 2, CB, 3, 4], BF16)
        mrow = sb("mrow", [12, 2, S], BF16)
        denom = sb("denom", [P, S])
        swapped = sb("swapped", [P, P])
        wdn_flat = wdn[:, :, :, :, :].rearrange("p a e k d -> p (a e k d)")
        NGB = 4
        gb = [m[:, i * TOPK * D:(i + 1) * TOPK * D].rearrange("p (k d) -> p k d", k=TOPK)
              for m in (wdn_flat, wgu_mem) for i in range(NGB // 2)]
        ysum = wdn_flat[:, 2 * TOPK * D:(2 * TOPK + 1) * D]
        pmax = [bank(f"pmax{i}") for i in range(2)]
        psc = [bank(f"psc{i}") for i in range(2)]
        pv = [bank(f"pv{i}") for i in range(2)]
        pD = pv[1]
        ring = [bank(f"ring{i}") for i in range(2)] + psc + pv[0:1]

        id_in = sem("id_in"); c_in = sem("c_in"); w_in = sem("w_in"); sw_in = sem("sw_in")
        x_in = [sem(f"x_in{b}") for b in range(B)]
        xn_out = sem("xn_out")
        const_b = sem("const_b"); rsum_ready = sem("rsum_ready"); pool_set = sem("pool_set");
        var_ready = sem("var_ready"); std_ready = sem("std_ready")
        xn_ready = sem("xn_ready")
        ring_full = sem("ring_full"); act_emptied = sem("act_emptied"); dve_emptied = sem("dve_emptied")
        mask_ready = sem("mask_ready"); negtop_ready = sem("negtop_ready"); ex_ready = sem("ex_ready")
        cum_ready = sem("cum_ready"); onehot_ready = sem("onehot_ready"); onehot_used = sem("onehot_used")
        taken = sem("taken")
        pos1_ready = sem("pos1_ready")
        weights_ready = sem("weights_ready"); got_ready = sem("got_ready")
        slots_ready = sem("slots_ready"); tok_ready = sem("tok_ready")
        xg_in = [sem(f"xg_in{i}") for i in range(4)]
        wgu_in = [sem(f"wgu_in{i}") for i in range(2)]
        wdn_in = [sem(f"wdn_in{i}") for i in range(2)]
        tanh_ready = sem("tanh_ready"); hx_ready = sem("hx_ready")
        y_out = [sem(f"y_out{i}") for i in range(2)]
        z_out = sem("z_out")
        tsh_ready = sem("tsh_ready")
        rot_ready = sem("rot_ready"); parts_ready = sem("parts_ready")
        parts_out = sem("parts_out")
        qk_in = [sem(f"qk_in{i}") for i in range(2)]
        max_full = sem("max_full"); max_emptied = sem("max_emptied"); mp_ready = sem("mp_ready")
        m_in = [sem(f"m_in{i}") for i in range(2)]
        sc_full = sem("sc_full"); exp_done = sem("exp_done")
        pv_done = sem("pv_done"); norm_done = sem("norm_done")
        gb_in = [sem(f"gb_in{i}") for i in range(NGB)]
        gb_used = sem("gb_used"); acc_done = sem("acc_done"); out_done = sem("out_done")
        dve_chain = sem("dve_chain"); pool_chain = sem("pool_chain")

        def emptied(eng, stage, k=None):
            n = FILL[stage] + (RING[stage[0]][0] - 1 if k is None else k)
            engine, count = EMPTIED[n]
            eng.wait_ge(act_emptied if engine == "act" else dve_emptied, count)

        def filled(eng, stage, k=0):
            n = FILL[stage] + k
            eng.wait_ge(ring_full, n + 1)
            return ring[BANKS[n]]

        order = {}
        for kind, arg in SCHED:
            order[(kind, arg)] = sum(1 for k2, _ in order if k2 == kind)

        ident = cst[:, C_ID:C_ID + P]
        tri = cstb[:, 0:P]
        mask_qk = cstb[:, P:2 * P]
        mask_kq = cstb[:, 2 * P:3 * P]
        ids = cstb[:, 3 * P:3 * P + 2 * NC].rearrange("p (c t) -> p c t", t=2)
        cosT = cst[:, C_COS:C_COS + S]
        low, high = cst[:, C_HALF:C_HALF + 1], cst[:, C_HALF + 1:C_HALF + 2]
        sinT = cst[:, C_SIN:C_SIN + S]
        x_v = x.rearrange("b (c p) d -> b p c d", p=P)
        xn_v = xn_rows.rearrange("(b c p) d -> b p c d", p=P, c=CB)
        out_v = out.rearrange("b (c p) d -> b c p d", p=P)

        def acc_count(c, kind):
            n = 0
            for k2, a2 in SCHED:
                if k2 in ("fin", "fsh", "comb"):
                    n += 1
                    if k2 == kind and a2 == c:
                        return n

        def split(engine, link, i):
            link(engine.tensor_add(rot1[:, i, :], rot1[:, i, :], rot2[:, i, :]))
            link(engine.tensor_copy(parts[:, i, 0, :], rot1[:, i, :]))
            link(engine.tensor_tensor(rot1[:, i, :], rot1[:, i, :], parts[:, i, 0, :], ALU.subtract))
            link(engine.tensor_copy(parts[:, i, 1, :], rot1[:, i, :]))
            engine.tensor_tensor(parts[:, i, 2, :], rot1[:, i, :], parts[:, i, 1, :], ALU.subtract
                                 ).then_inc(parts_ready, 1)

        def split_count(a):
            return 2 * (a + 1)

        block = ctx.enter_context(nc.Block())

        @block.sync
        def _(sp):
            sp.dma_start(acc[:, 0:CB, :], x_v[0]).then_inc(x_in[0], 16)
            sp.dma_start(cst[:, 0:C_COS], const[:, 0:C_COS]).then_inc(id_in, 16)
            for i, w in enumerate((wq, wk, wv, wo)):
                sp.dma_start(wraw[:, i, :, :], w.rearrange("(o p) d -> p o d", p=P)).then_inc(w_in, 16)
            sp.dma_start(graw[:, :], gate_w).then_inc(w_in, 16)
            for b in range(1, B):
                sp.dma_start(acc[:, CB * b:CB * b + CB, :], x_v[b]).then_inc(x_in[b], 16)
                if b == 1:
                    sp.dma_start(cst[:, C_COS:C_END], const[:, C_COS:C_END]).then_inc(c_in, 16)
            sp.dma_start(swg[:, :, :], sw_gate.rearrange("(p k) i -> p k i", k=2)).then_inc(sw_in, 16)
            sp.dma_start(swu[:, :, :], sw_up.rearrange("(p k) i -> p k i", k=2)).then_inc(sw_in, 16)
            for m, (m0, mw) in enumerate(SM):
                sp.dma_start(swd[0:mw, m, :], sw_down[m0:m0 + mw, :]).then_inc(sw_in, 16)

            def load_experts(G):
                buf = G % 2
                if G >= 2:
                    emptied(sp, ("gu", G - 2))
                elif G == 0:
                    sp.wait_ge(slots_ready, 1)
                    sp.wait_ge(onehot_ready, 4)
                for i, w in enumerate((w_gate, w_up)):
                    sp.dma_start(wgu[:, buf, i, :, :, :].rearrange("p e k i -> p e (k i)"),
                                 w[EG * G:EG * G + EG].rearrange("e (p k) i -> p e (k i)", k=2)
                                 ).then_inc(wgu_in[buf], 16)
                if G >= 2:
                    emptied(sp, ("dn", G - 2))
                else:
                    sp.wait_ge(onehot_used, 4)
                sp.dma_start(wdn[0:IH, buf, :, :, :].rearrange("p e k d -> p e (k d)"),
                             w_down[EG * G:EG * G + EG].rearrange("e (p k) d -> p e (k d)", k=2)
                             ).then_inc(wdn_in[buf], 16)

            for kind, a in SCHED:
                if kind == "lg" and a == NC - 1:
                    for b in range(B):
                        sp.wait_ge(xn_ready, CB * (b + 1))
                        sp.dma_start(xn_v[b], xn[:, CB * b:CB * b + CB, :]).then_inc(xn_out, 16)
                elif kind == "slots":
                    load_experts(0)
                    load_experts(1)
                    sp.wait_ge(pool_set, 1)
                    sp.dma_start(y_rows[0:1, :], zrow[:, :]).then_inc(z_out, 16)
                elif kind == "proj" and a[1] == 1:
                    a = a[0]
                    buf = a % 2
                    sp.wait_ge(parts_ready, split_count(a))
                    if a >= 2:
                        sp.wait_ge(qk_in[buf], 9 * 16 * (a // 2))
                    for i in range(2):
                        for t in range(3):
                            sp.dma_start(parts_d[buf, i, t].rearrange("d h n -> h d n"),
                                         parts[:, i, t, :]).then_inc(parts_out, 16)
                elif kind == "qk":
                    buf = a % 2
                    sp.wait_ge(parts_out, 6 * 16 * (a + 1))
                    if a >= 2:
                        sp.wait_ge(sc_full, NF * (2 * a - 2))
                    for t, src in enumerate((0, 0, 0, 1, 1, 2)):
                        sp.dma_start(q6[DK * t:DK * t + DK, buf, :, :], parts_d[buf, 0, src]
                                     ).then_inc(qk_in[buf], 16)
                    for t0, n in ((0, 3), (3, 2), (5, 1)):
                        sp.dma_start(k6[DK * t0:DK * (t0 + n), buf, :, :],
                                     parts_d[buf, 1, 0:n].rearrange("t d h n -> (t d) h n")
                                     ).then_inc(qk_in[buf], 16)
                elif kind == "dn":
                    emptied(sp, ("dn", a))
                    sp.dma_start(y_rows[1 + P * a:1 + P * a + P, :], ys[:, a % 2, :]).then_inc(y_out[a % 2], 16)
                    if a + 2 < NG:
                        load_experts(a + 2)
                elif kind == "store":
                    sp.wait_ge(acc_done, max(acc_count(a, "fin"), acc_count(a, "comb")))
                    sp.dma_start(out_v[a // CB, a % CB], acc[:, a, :]).then_inc(out_done, 16)
            sp.wait_ge(out_done, 16 * NC)

        @block.gpsimd
        def _(pool):
            links = [0]

            def link(ins):
                links[0] += 1
                ins.then_inc(pool_chain, 1)
                pool.wait_ge(pool_chain, links[0])

            nc.gpsimd.memset(zrow[:, :], 0.0).then_inc(pool_set, 1)
            nc.gpsimd.memset(onesb[:, :], 1.0).then_inc(pool_set, 1)
            emptied(pool, ("wT", 3))
            nc.gpsimd.memset(L[:, :, E:E + 2], BIG).then_inc(pool_set, 1)
            pool.wait_ge(pool_set, 3)
            nc.gpsimd.memset(k6[KQ:P, :, :, :], 1.0).then_inc(pool_set, 1)
            pool.wait_ge(pool_set, 4)
            nc.gpsimd.memset(cum[:, 0, :], 0.0).then_inc(pool_set, 1)
            def gather_tokens(G):
                if G >= 4:
                    emptied(pool, ("xg", G - 4))
                pool.indirect_dma_start(out=xg[:, G % 4, :], out_offset=None, in_=xn_rows,
                                        in_offset=bass.IndirectOffsetOnAxis(ap=toku[:, G:G + 1], axis=0)
                                        ).then_inc(xg_in[G % 4], 16)

            for kind, a in SCHED:
                if kind == "proj" and a != (0, 1):
                    u, i = a
                    pool.wait_ge(rot_ready, 2 * u + i + 1)
                    if u >= 1 and i == 0:
                        pool.wait_ge(parts_out, 6 * 16 * u)
                    split(nc.gpsimd, link, i)
                elif kind == "weights":
                    pool.wait_ge(rsum_ready, 1)
                    rb = rsum[:, :].rearrange("p (c o) -> p c o", o=1).broadcast_to([P, NC, E])
                    link(nc.gpsimd.tensor_tensor(ex[:, :, :], ex[:, :, :], rb, ALU.mult))
                    exg = ex[:, :, :].rearrange("p c (g e) -> p (c g) e", e=EG)
                    dg = disp[:, :, :, :].rearrange("p c g n -> p (c g) n")
                    part = [dg[:, :, 2 + EG * t:2 + EG * t + EG] for t in range(3)]
                    link(nc.gpsimd.tensor_copy(part[0], exg))
                    link(nc.gpsimd.tensor_tensor(exg, exg, part[0], ALU.subtract))
                    link(nc.gpsimd.tensor_copy(part[1], exg))
                    link(nc.gpsimd.tensor_tensor(part[2], exg, part[1], ALU.subtract))
                    idb = ids.rearrange("p c (o t) -> p c o t", o=1).broadcast_to([P, NC, NG, 2])
                    pool.wait_ge(const_b, 2)
                    nc.gpsimd.tensor_copy(disp[:, :, :, 0:2], idb).then_inc(weights_ready, 1)
                elif kind == "disp":
                    pool.wait_ge(tok_ready, 1)
                    pool.wait_ge(onehot_used, 4)
                    for G in range(4):
                        gather_tokens(G)
                elif kind == "xT" and a == NC - 1:
                    pool.wait_ge(xn_out, 16 * B)
                    emptied(pool, (kind, a))
                    nc.gpsimd.memset(vhat[:, :, :, :], 1.0).then_inc(pool_set, 1)
                elif kind == "xg" and a + 4 < NG:
                    gather_tokens(a + 4)
                elif kind == "gather":
                    if a == 0:
                        pool.wait_ge(slots_ready, 1)
                        pool.wait_ge(z_out, 16)
                        for i in range(2):
                            pool.wait_ge(y_out[i], 16 * (NG // 2))
                    if a >= NGB:
                        pool.wait_ge(gb_used, a - NGB + 1)
                    for k in range(TOPK):
                        pool.indirect_dma_start(out=gb[a % NGB][:, k, :], out_offset=None, in_=y_rows,
                                                in_offset=bass.IndirectOffsetOnAxis(
                                                    ap=slotu[:, a, k:k + 1], axis=0)
                                                ).then_inc(gb_in[a % NGB], 16)

        @block.scalar
        def _(act):
            act.wait_ge(id_in, 16)
            nc.scalar.activation(identb[:, :], ident, ACT.Copy).then_inc(const_b, 1)
            tanhs = 0
            for kind, a in SCHED:
                if kind == "wT":
                    r = filled(act, (kind, a))
                    if a < 4:
                        nc.scalar.activation(wT[:, a, :, :].rearrange("p k d -> p (k d)"), r[:, :],
                                             ACT.Copy).then_inc(act_emptied, 1)
                    else:
                        nc.scalar.activation(gT[:, :, :].rearrange("p k e -> p (k e)"), r[:, 0:2 * E],
                                             ACT.Copy).then_inc(act_emptied, 1)
                elif kind == "ln":
                    act.wait_ge(var_ready, a + 1)
                    nc.scalar.activation(std[:, a, :], vareps[:, a, :], ACT.Sqrt).then_inc(std_ready, 1)
                elif kind == "xT":
                    r = filled(act, (kind, a))
                    nc.scalar.activation(xnT[:, :, P * a:P * a + P],
                                         r[:, 0:2 * P].rearrange("p (k t) -> p k t", k=2),
                                         ACT.Copy).then_inc(act_emptied, 1)
                elif kind == "lg":
                    r = filled(act, (kind, a))
                    nc.scalar.activation(L[:, a, 0:E], r[:, 0:E], ACT.Copy).then_inc(act_emptied, 1)
                elif kind == "qk" and a == 0:
                    act.wait_ge(c_in, 16)
                    nc.scalar.activation(cstb[:, :], cst[:, C_TRI:C_END], ACT.Copy).then_inc(const_b, 1)
                elif kind == "route":
                    act.wait_ge(negtop_ready, 1)
                    emptied(act, ("lg", NC - 1))
                    for c in range(NC):
                        nc.scalar.activation(ex[:, c, :], L[:, c, 0:E], ACT.Exp, bias=negtop[:, c:c + 1],
                                             accum_out=exsum[:, c:c + 1]).then_inc(ex_ready, 1)
                elif kind == "V":
                    b, i = a
                    if b == 0:
                        act.wait_ge(pool_set, 6)
                    else:
                        act.wait_ge(pv_done, CB * 4 * b)
                    r = filled(act, (kind, a))[:, :].rearrange("p (c h2 e d) -> p c h2 e d", c=2, e=2, d=DK)
                    vv = vhat[:, 2 * i:2 * i + 2, :, :].rearrange("p c (h2 e) w -> p c h2 e w", e=2)
                    for cc in range(2):
                        for e in range(2):
                            last = nc.scalar.activation(vv[:, cc, :, e, DK * e:DK * e + DK],
                                                        r[:, cc, :, e, :], ACT.Copy)
                    last.then_inc(act_emptied, 1)
                elif kind == "take":
                    b, blk = a // 2, a % 2
                    act.wait_ge(pv_done, CB * (2 * a + 1))
                    if b >= 1 and blk == 0:
                        emptied(act, ("fin", CB * b - 1))
                    if a >= 1:
                        act.wait_ge(norm_done, CB * a)
                    nc.scalar.activation(denom[:, :], pv[0][:, :], ACT.Copy, scale=high)
                    nc.scalar.activation(aT[:, blk, :], pv[0][:, :], ACT.Copy, scale=low).then_inc(taken, 1)
                elif kind == "mT":
                    if a >= 2:
                        act.wait_ge(m_in[a % 2], 48 * (a // 2))
                    r = filled(act, (kind, a))
                    nc.scalar.activation(mrow[:, a % 2, :], r[:, :].bitcast(BF16)[0:12, 0:S],
                                         ACT.Copy).then_inc(act_emptied, 1)
                    emptied(act, (kind, a))
                    for t in range(3):
                        act.dma_start(q6[KQ + t:KQ + t + 1, a // 2 % 2, a % 2::2, :],
                                      mrow[4 * t:4 * t + 4, a % 2, :]).then_inc(m_in[a % 2], 16)
                elif kind == "att" and 1 <= a[0] <= NA:
                    g = a[0] - 1
                    for i in within(EXP_E, a[1]):
                        kc, h0, n = SECOND[i]
                        act.wait_ge(sc_full, NF * g + i + 1)
                        if g >= 1:
                            act.wait_ge(pv_done, CB * (g - 1) + kc + 1)
                        w = S - P * kc
                        o = PT_OFF[kc] + h0 * w
                        nc.scalar.activation(probs[:, o:o + n * w], psc[(NF * g + i) % 2][:, 0:n * w],
                                             ACT.Exp, scale=DK ** -0.5).then_inc(exp_done, 1)
                elif kind == "xg":
                    r = filled(act, (kind, a))
                    if a >= 2:
                        emptied(act, ("gu", a - 2))
                    nc.scalar.activation(xgT[:, a % 2, :, :].rearrange("p k t -> p (k t)"), r[:, 0:2 * P],
                                         ACT.Copy).then_inc(act_emptied, 1)
                elif kind == "gu":
                    r = filled(act, (kind, a))
                    if a >= 1:
                        emptied(act, ("gu", a - 1))
                    nc.scalar.activation(th[:, :], r[:, 0:I], ACT.Tanh, scale=0.5).then_inc(tanh_ready, 1)
                elif kind == "aT":
                    r = filled(act, (kind, a))
                    nc.scalar.activation(hxT[:, :, :].rearrange("p k t -> p (k t)"), r[0:IH, 0:2 * P],
                                         ACT.Copy).then_inc(act_emptied, 1)
                elif kind == "wperm":
                    r = filled(act, (kind, a))
                    nc.scalar.activation(wslot[:, :], r[:, 0:NG], ACT.Copy).then_inc(act_emptied, 1)
                elif kind == "dn":
                    r = filled(act, (kind, a))
                    if a == 0:
                        emptied(act, ("wperm", 0))
                    if a >= 2:
                        act.wait_ge(y_out[a % 2], 16 * (a // 2))
                    nc.scalar.activation(ys[:, a % 2, :], r[:, 0:D], ACT.Copy,
                                         scale=wslot[:, a:a + 1]).then_inc(act_emptied, 1)
                elif kind == "sh" and a[2] == 0:
                    m0, mw = SM[a[1]]
                    r = filled(act, (kind, a))
                    tanhs += 1
                    if tanhs >= 2:
                        emptied(act, last_sh)
                    last_sh = (kind, a)
                    nc.scalar.activation(tsh[0:mw, :], r[0:mw, :], ACT.Tanh, scale=0.5).then_inc(tsh_ready, 1)

        @block.vector
        def _(dve):
            links = [0]

            def link(ins):
                links[0] += 1
                ins.then_inc(dve_chain, 1)
                dve.wait_ge(dve_chain, links[0])

            def variances(b):
                dve.wait_ge(x_in[b], 16)
                for c in range(CB):
                    last = nc.vector.bn_stats(st6[:, b, c, :], acc[:, CB * b + c, :])
                link(last)
                for c in range(CB):
                    last = nc.vector.bn_aggr(mv[:, b, c, :], st6[:, b, c, :])
                link(last)
                nc.vector.tensor_scalar(vareps[:, b, :], mv[:, b, :, 1], EPS, None, ALU.add).then_inc(var_ready, 1)

            shs = 0
            for kind, a in SCHED:
                if kind == "ln":
                    for b in ((0,), (1, 2), (3,), ())[a]:
                        variances(b)
                    dve.wait_ge(std_ready, a + 1)
                    link(nc.vector.reciprocal(rstd[:, a, :], std[:, a, :]))
                    link(nc.vector.tensor_tensor(newton[:, a, :], vareps[:, a, :], rstd[:, a, :], ALU.mult))
                    link(nc.vector.tensor_tensor(newton[:, a, :], newton[:, a, :], rstd[:, a, :], ALU.mult))
                    link(nc.vector.tensor_scalar(newton[:, a, :], newton[:, a, :], -0.5, 1.5, ALU.mult, ALU.add))
                    link(nc.vector.tensor_tensor(rstd[:, a, :], rstd[:, a, :], newton[:, a, :], ALU.mult))
                    for c in range(CB):
                        nc.vector.tensor_scalar(xn[:, CB * a + c, :], acc[:, CB * a + c, :], mv[:, a, c, 0:1],
                                                rstd[:, a, c:c + 1], ALU.subtract, ALU.mult).then_inc(xn_ready, 1)
                elif kind == "route":
                    emptied(dve, ("lg", NC - 1))
                    dve.wait_ge(pool_set, 5)
                    for c in range(NC):
                        last = nc.vector.max(top8[:, c, :], L[:, c, :])
                    link(last)
                    nc.vector.tensor_scalar(negtop[:, :], top8[:, :, 2], -1.0, None, ALU.mult).then_inc(negtop_ready, 1)
                    for c in range(NC):
                        last = nc.vector.match_replace(Lrep[:, c, :], top8[:, c, :], L[:, c, :], -BIG)
                    link(last)
                    nc.vector.tensor_tensor(mask[:, :, :], L[:, :, 0:E], Lrep[:, :, 0:E], ALU.is_gt
                                            ).then_inc(mask_ready, 1)
                    dve.wait_ge(mask_ready, 1)
                    for c in range(1, NC):
                        nc.vector.tensor_tensor(cum[:, c, :], cum[:, c - 1, :], mask[:, c - 1, :], ALU.add
                                                ).then_inc(cum_ready, 1)
                        dve.wait_ge(cum_ready, c)
                elif kind == "pos":
                    if a == 0:
                        dve.wait_ge(ex_ready, NC)
                        dve.wait_ge(c_in, 16)
                    r = filled(dve, (kind, a))[:, :].rearrange("p (c e) -> p c e", e=E)
                    cs = slice(8 * a, 8 * a + 8)
                    base = cst[:, C_BASE:C_BASE + E].rearrange("p (o e) -> p o e", o=1).broadcast_to([P, 8, E])
                    link(nc.vector.scalar_tensor_tensor(valid[:, cs, :], r, float(CAP), mask[:, cs, :],
                                                        ALU.is_lt, ALU.mult))
                    nc.vector.tensor_tensor(key[:, cs, :], r, base, ALU.add)
                    nc.vector.scalar_tensor_tensor(pos1[:, cs, :], r, 1.0, valid[:, cs, :],
                                                   ALU.add, ALU.mult).then_inc(dve_emptied, 1)
                    emptied(dve, (kind, a))
                    dve.sem_inc(pos1_ready, 1)
                    link(nc.vector.tensor_tensor(key[:, cs, :], key[:, cs, :], valid[:, cs, :], ALU.mult))
                elif kind == "weights":
                    dve.wait_ge(ex_ready, NC)
                    nc.vector.reciprocal(rsum[:, :], exsum[:, :]).then_inc(rsum_ready, 1)
                elif kind == "hot":
                    if a >= 1:
                        dve.wait_ge(onehot_used, a)
                    src = pos1[:, 4 * a:4 * a + 4, :].rearrange("p c (g e) -> p (c g) e", e=EG)
                    for k in range(CAP):
                        last = nc.vector.tensor_scalar(onehot[:, :, k, :], src, float(k + 1), None, ALU.is_equal)
                    last.then_inc(onehot_ready, 1)
                elif kind == "disp":
                    dve.wait_ge(onehot_used, 4)
                    link(nc.vector.tensor_copy(got[:, :, :].rearrange("p g n -> p (g n)"), pD[:, 0:NG * NDV]))
                    link(nc.vector.scalar_tensor_tensor(tokf[:, :], got[:, :, 0], float(P), got[:, :, 1],
                                                        ALU.mult, ALU.add))
                    nc.vector.tensor_copy(toku[:, :], tokf[:, :]).then_inc(tok_ready, 1)
                    link(nc.vector.tensor_tensor(w3[:, :, :], got[:, :, 2:2 + EG], got[:, :, 2 + EG:2 + 2 * EG],
                                                 ALU.add))
                    link(nc.vector.tensor_tensor(w3[:, :, :], w3[:, :, :], got[:, :, 2 + 2 * EG:NDV], ALU.add))
                    own = cst[:, C_OWN:C_OWN + EG].rearrange("p (o e) -> p o e", o=1).broadcast_to([P, NG, EG])
                    link(nc.vector.tensor_tensor(w3[:, :, :], w3[:, :, :], own, ALU.mult))
                    nc.vector.tensor_reduce(wgot[:, :], w3[:, :, :], AX.X, ALU.add).then_inc(tok_ready, 1)
                elif kind == "slots":
                    for c in range(NC):
                        last = nc.vector.max(slot8[:, c, :], key[:, c, :])
                    link(last)
                    nc.vector.tensor_copy(slotu[:, :, :], slot8[:, :, :]).then_inc(slots_ready, 1)
                elif kind == "proj":
                    u, i = a
                    if u == 0:
                        dve.wait_ge(c_in, 16)
                    elif i == 0:
                        dve.wait_ge(parts_ready, split_count(u - 1))
                    r = filled(dve, (kind, a))
                    nc.vector.tensor_tensor(rot1[:, i, :], r[:, :], cosT, ALU.mult)
                    nc.vector.stream_shuffle(rot2[:, i, :], r[:, :], [j ^ 1 for j in range(32)]
                                             ).then_inc(dve_emptied, 1)
                    emptied(dve, (kind, a))
                    nc.vector.tensor_tensor(rot2[:, i, :], rot2[:, i, :], sinT, ALU.mult).then_inc(rot_ready, 1)
                    if a == (0, 1):
                        dve.wait_ge(rot_ready, 2)
                        split(nc.vector, link, 1)
                elif kind == "att" and a[0] < NA:
                    g, e = a
                    for i in within(MAX_E, e):
                        qc, h0, n = FIRST[i]
                        w = P * (qc + 1)
                        dve.wait_ge(max_full, NF * g + i + 1)
                        r = pmax[(NF * g + i) % 2][:, 0:n * w].rearrange("p (h w) -> p h w", h=n)
                        nc.vector.tensor_reduce(mx[:, qc, h0:h0 + n], r, AX.X, ALU.max).then_inc(max_emptied, 1)
                    if e < 15:
                        continue
                    dve.wait_ge(max_emptied, NF * (g + 1))
                    if g >= 2:
                        emptied(dve, ("mT", g - 2))
                    m = mp[:, g % 2, :, :, :]
                    link(nc.vector.tensor_scalar(m[:, :, 0, :], mx[:, :, :], -1.0, None, ALU.mult))
                    link(nc.vector.scalar_tensor_tensor(mres[:, :, :], mx[:, :, :], -1.0, m[:, :, 0, :],
                                                        ALU.mult, ALU.subtract))
                    link(nc.vector.tensor_copy(m[:, :, 1, :], mres[:, :, :]))
                    nc.vector.tensor_tensor(m[:, :, 2, :], mres[:, :, :], m[:, :, 1, :],
                                            ALU.subtract).then_inc(mp_ready, 1)
                    dve.wait_ge(mp_ready, g + 1)
                elif kind == "gu":
                    r = filled(dve, (kind, a))
                    dve.wait_ge(tanh_ready, a + 1)
                    if a >= 1:
                        emptied(dve, ("aT", a - 1))
                    link(nc.vector.scalar_tensor_tensor(ga[:, :], th[:, :], 1.0, r[:, 0:I], ALU.add, ALU.mult))
                    nc.vector.scalar_tensor_tensor(hx[:, :], ga[:, :], 0.5, r[:, I:2 * I], ALU.mult, ALU.mult
                                                   ).then_inc(dve_emptied, 1)
                    emptied(dve, (kind, a))
                elif kind == "sh":
                    b, m, i = a
                    mw = SM[m][1]
                    if i == 0:
                        shs += 1
                        dve.wait_ge(tsh_ready, shs)
                        r = filled(dve, (kind, a))
                        nc.vector.scalar_tensor_tensor(gsh[0:mw, :], tsh[0:mw, :], 1.0, r[0:mw, :],
                                                       ALU.add, ALU.mult).then_inc(dve_emptied, 1)
                        emptied(dve, (kind, a))
                        continue
                    if b >= 1 and m == 0:
                        emptied(dve, ("fin", CB * b - 1))
                    r = filled(dve, (kind, a))
                    nc.vector.scalar_tensor_tensor(hT[0:mw, m, :], gsh[0:mw, :], 0.5, r[0:mw, :],
                                                   ALU.mult, ALU.mult).then_inc(dve_emptied, 1)
                    emptied(dve, (kind, a))
                elif kind == "norm":
                    u, q = a
                    qs = slice(P * q, P * q + P)
                    if u == NU - 1:
                        dve.wait_ge(pv_done, CB * (NA - 1) + q + 1)
                    elif q == 0:
                        dve.wait_ge(pv_done, CB * (2 * u + 2))
                    if q == 0:
                        dve.wait_ge(taken, u + 1)
                    link(nc.vector.scalar_tensor_tensor(denom[:, qs], pv[1][:, qs], low, denom[:, qs],
                                                        ALU.mult, ALU.add))
                    link(nc.vector.stream_shuffle(swapped[:, :], denom[:, qs], [j ^ DK for j in range(32)]))
                    nc.vector.scalar_tensor_tensor(aT[:, u % 2, qs], pv[1][:, qs], high, aT[:, u % 2, qs],
                                                   ALU.mult, ALU.add)
                    link(nc.vector.reciprocal(swapped[:, :], swapped[:, :]))
                    nc.vector.tensor_tensor(aT[:, u % 2, qs], aT[:, u % 2, qs], swapped[:, :], ALU.mult
                                            ).then_inc(norm_done, 1)
                    dve.wait_ge(norm_done, CB * u + q + 1)
                elif kind in ("fin", "fsh"):
                    r = filled(dve, (kind, a))
                    dve.wait_ge(xn_ready, NC)
                    link(nc.vector.tensor_tensor(acc[:, a, :], acc[:, a, :], r[:, 0:D], ALU.add))
                    dve.sem_inc(dve_emptied, 1)
                    dve.sem_inc(acc_done, 1)
                elif kind == "comb":
                    dve.wait_ge(gb_in[a % NGB], TOPK * 16 * (a // NGB + 1))
                    nc.vector.tensor_reduce(ysum[:, :], gb[a % NGB].rearrange("p k d -> p d k"), AX.X,
                                            ALU.add).then_inc(gb_used, 1)
                    dve.wait_ge(gb_used, a + 1)
                    link(nc.vector.tensor_tensor(acc[:, a, :], acc[:, a, :], ysum[:, :], ALU.add))
                    dve.sem_inc(acc_done, 1)

        @block.tensor
        def _(pe):
            def wait_emptied(n):
                engine, count = EMPTIED[n]
                pe.wait_ge(act_emptied if engine == "act" else dve_emptied, count)

            def claim(stage, k=0):
                n = FILL[stage] + k
                if BEFORE[n] is not None:
                    wait_emptied(BEFORE[n])
                return ring[BANKS[n]]

            def scores_for_max(g, i):
                u, hg = g // 2, g % 2
                qc, h0, n = FIRST[i]
                f = NF * g + i
                if f >= 2:
                    pe.wait_ge(max_emptied, f - 1)
                w = P * (qc + 1)
                for j in range(n):
                    h = 2 * (h0 + j) + hg
                    o = pmax[f % 2][:, w * j:w * j + w]
                    nc.tensor.matmul(o, q6[0:KQ, u % 2, h, P * qc:P * qc + P], k6[0:KQ, u % 2, h, 0:w],
                                     start=True, stop=False)
                    last = nc.tensor.matmul(o[:, w - P:w], identb[:, :], mask_qk, start=False, stop=True)
                last.then_inc(max_full, 1)

            def scores_for_exp(g, i):
                u, hg = g // 2, g % 2
                kc, h0, n = SECOND[i]
                f = NF * g + i
                if f >= 2:
                    pe.wait_ge(exp_done, f - 1)
                w = S - P * kc
                for j in range(n):
                    h = 2 * (h0 + j) + hg
                    o = psc[f % 2][:, w * j:w * j + w]
                    nc.tensor.matmul(o, k6[0:KM, u % 2, h, P * kc:P * kc + P], q6[0:KM, u % 2, h, P * kc:S],
                                     start=True, stop=False)
                    last = nc.tensor.matmul(o[:, 0:P], identb[:, :], mask_kq, start=False, stop=True)
                last.then_inc(sc_full, 1)

            def values_begin(g):
                u, hg = g // 2, g % 2
                emptied(pe, ("V", (u // 2, 1)))
                if u >= 1 and hg == 0:
                    pe.wait_ge(taken, u)
                elif u >= 1:
                    pe.wait_ge(norm_done, CB * u)

            def values(g, kc, j):
                u, hg = g // 2, g % 2
                w = S - P * kc
                if j == 0:
                    pe.wait_ge(exp_done, NF * g + max(i for i in range(NF) if SECOND[i][0] == kc) + 1)
                o = PT_OFF[kc] + w * j
                last = nc.tensor.matmul(pv[hg][32 * j:32 * j + 32, P * kc:S],
                                        vhat[:, kc, HB * (u % 2) + 2 * j + hg, :], probs[:, o:o + w],
                                        start=(kc == 0), stop=(kc == CB - 1), skip_group_check=True)
                if j == 3:
                    last.then_inc(pv_done, 1)

            pe.wait_ge(id_in, 16)
            pe.wait_ge(w_in, 5 * 16)
            for kind, a in SCHED:
                if kind == "wT":
                    r = claim((kind, a))
                    for k in range(2):
                        if a == 4:
                            last = nc.tensor.transpose(r[:, E * k:E * k + E], graw[:, k::2], ident[0:E, 0:E])
                            continue
                        for o in range(2):
                            src = wraw[:, a, o, k::2] if a < 3 else wraw[:, a, o, P * k:P * k + P]
                            last = nc.tensor.transpose(r[:, D * k + P * o:D * k + P * o + P], src, ident)
                    last.then_inc(ring_full, 1)
                elif kind == "xT":
                    r = claim((kind, a))
                    pe.wait_ge(xn_ready, a + 1)
                    for k in range(2):
                        last = nc.tensor.transpose(r[:, P * k:P * k + P], xn[:, a, k::2], ident)
                    last.then_inc(ring_full, 1)
                elif kind == "lg":
                    r = claim((kind, a))
                    emptied(pe, ("xT", a))
                    for k in range(2):
                        last = nc.tensor.matmul(r[:, 0:E], xnT[:, k, P * a:P * a + P], gT[:, k, :],
                                                start=(k == 0), stop=(k == 1))
                    last.then_inc(ring_full, 1)
                elif kind == "pos":
                    r = claim((kind, a))
                    pe.wait_ge(const_b, 2)
                    pe.wait_ge(pool_set, 2)
                    pe.wait_ge(cum_ready, NC - 1)
                    for c in range(8 * a, 8 * a + 8):
                        o = r[:, E * (c % 8):E * (c % 8) + E]
                        nc.tensor.matmul(o, tri, mask[:, c, :], start=True, stop=False)
                        last = nc.tensor.matmul(o, onesb[:, :], cum[:, c, :], start=False, stop=True)
                    last.then_inc(ring_full, 1)
                elif kind == "oh":
                    pe.wait_ge(weights_ready, 1)
                    pe.wait_ge(onehot_ready, a + 1)
                    for c in range(4 * a, 4 * a + 4):
                        for G in range(NG):
                            last = nc.tensor.matmul(
                                pD[:, NDV * G:NDV * G + NDV],
                                onehot[:, (c % 4) * NG + G, :, :].rearrange("p k e -> p (k e)"), disp[:, c, G, :],
                                start=(c == 0 and G == 0), stop=(c == NC - 1), skip_group_check=True)
                    last.then_inc(onehot_used, 1)
                elif kind == "wperm":
                    r = claim((kind, a))
                    pe.wait_ge(tok_ready, 2)
                    nc.tensor.matmul(r[:, 0:NG], cst[:, C_PERM:C_PERM + P], wgot[:, :], start=True, stop=True
                                     ).then_inc(ring_full, 1)
                elif kind == "proj":
                    u, i = a
                    b, blk = u // 2, u % 2
                    emptied(pe, ("xT", CB * (b + 1) - 1))
                    r = claim((kind, a))
                    for k in range(2):
                        last = nc.tensor.matmul(r[:, :], wT[:, i, k, P * blk:P * blk + P],
                                                xnT[:, k, S * b:S * b + S], start=(k == 0), stop=(k == 1))
                    last.then_inc(ring_full, 1)
                elif kind == "V":
                    b, i = a
                    r = claim((kind, a))
                    for cc in range(2):
                        c = CB * b + 2 * i + cc
                        for k in range(2):
                            last = nc.tensor.matmul(r[:, D * cc:D * cc + D], xnT[:, k, P * c:P * c + P],
                                                    wT[:, 2, k, :], start=(k == 0), stop=(k == 1))
                    last.then_inc(ring_full, 1)
                elif kind == "sh":
                    b, m, i = a
                    m0, mw = SM[m]
                    pe.wait_ge(sw_in, 5 * 16)
                    r = claim((kind, a))
                    w = (swg, swu)[i]
                    for k in range(2):
                        last = nc.tensor.matmul(r[0:mw, :], w[:, k, m0:m0 + mw], xnT[:, k, S * b:S * b + S],
                                                start=(k == 0), stop=(k == 1))
                    last.then_inc(ring_full, 1)
                elif kind == "att":
                    g, e = a
                    if a == (0, 0):
                        pe.wait_ge(const_b, 2)
                    if e == 0 and g < NA:
                        pe.wait_ge(qk_in[g // 2 % 2], 9 * 16 * (g // 4 + 1))
                    if e == EXP_E[0] and 1 <= g <= NA:
                        pe.wait_ge(m_in[(g - 1) % 2], 48 * ((g - 1) // 2 + 1))
                        if g == 1:
                            pe.wait_ge(pool_set, 4)
                            for n in range(EARLY_BANKS):
                                wait_emptied(LAST_EARLY - n)
                    if e == 0 and g >= 2:
                        values_begin(g - 2)
                    for i in within(MAX_E, e) if g < NA else ():
                        scores_for_max(g, i)
                    for i in within(VAL_E, e) if g >= 2 else ():
                        values(g - 2, i // 4, i % 4)
                    for i in within(EXP_E, e) if 1 <= g <= NA else ():
                        scores_for_exp(g - 1, i)
                elif kind == "mT":
                    r = claim((kind, a))
                    pe.wait_ge(mp_ready, a + 1)
                    for qc in range(CB):
                        last = nc.tensor.transpose(r[:, :].bitcast(BF16)[0:12, P * qc:P * qc + P],
                                                   mp[:, a % 2, qc, :, :].rearrange("p t h -> p (t h)"), identb[:, :])
                    last.then_inc(ring_full, 1)
                elif kind == "xg":
                    r = claim((kind, a))
                    pe.wait_ge(xg_in[a % 4], 16 * (a // 4 + 1))
                    for k in range(2):
                        last = nc.tensor.transpose(r[:, P * k:P * k + P], xg[:, a % 4, k::2], ident)
                    last.then_inc(ring_full, 1)
                elif kind == "gu":
                    r = claim((kind, a))
                    pe.wait_ge(wgu_in[a % 2], 32 * (a // 2 + 1))
                    emptied(pe, ("xg", a))
                    for k in range(2):
                        for j in range(EG):
                            last = nc.tensor.matmul(r[32 * j:32 * j + 32, 0:2 * I],
                                                    xgT[:, a % 2, k, j::EG],
                                                    wgu[:, a % 2, :, j, k, :], start=(k == 0), stop=(k == 1))
                    last.then_inc(ring_full, 1)
                elif kind == "aT":
                    r = claim((kind, a))
                    emptied(pe, ("gu", a))
                    if a >= 1:
                        emptied(pe, ("dn", a - 1))
                    for k in range(2):
                        last = nc.tensor.transpose(r[0:IH, P * k:P * k + P], hx[:, k::2], ident)
                    last.then_inc(ring_full, 1)
                elif kind == "dn":
                    r = claim((kind, a))
                    pe.wait_ge(wdn_in[a % 2], 16 * (a // 2 + 1))
                    emptied(pe, ("aT", a))
                    for k in range(2):
                        for j in range(EG):
                            last = nc.tensor.matmul(r[32 * j:32 * j + 32, 0:D], hxT[:, k, CAP * j:CAP * j + CAP],
                                                    wdn[0:IH, a % 2, j, k, :], start=(k == 0), stop=(k == 1))
                    last.then_inc(ring_full, 1)
                elif kind in ("fin", "fsh"):
                    b, cq = a // CB, a % CB
                    r = claim((kind, a))
                    products = []
                    if kind == "fin":
                        pe.wait_ge(norm_done, CB * (2 * b + 1) + (CB if b < B - 1 else cq + 1))
                        products += [(aT[:, blk, P * cq:P * cq + P], wT[:, 3, blk, :]) for blk in range(2)]
                    if kind == "fsh" or b < B - 1:
                        emptied(pe, ("sh", (b, 2, 1)))
                        products += [(hT[0:mw, m, P * cq:P * cq + P], swd[0:mw, m, :]) for m, (_, mw) in enumerate(SM)]
                    for i, (lhsT, rhs) in enumerate(products):
                        last = nc.tensor.matmul(r[:, 0:D], lhsT, rhs, start=(i == 0), stop=(i == len(products) - 1))
                    last.then_inc(ring_full, 1)


def constants(np):
    f = np.float32
    c = np.zeros((P, C_END), f)
    c[:, C_ID:C_ID + P] = np.eye(P, dtype=f)
    inv = f(10000.0) ** (f(-2.0) * np.arange(DK // 2, dtype=f) / f(DK))
    ang = (np.arange(S, dtype=f)[:, None] * inv[None, :].astype(f)).astype(f)
    row = (np.arange(P) % DK) // 2
    sign = np.where(np.arange(P) % 2 == 0, f(-1), f(1))
    c[:, C_COS:C_COS + S] = np.cos(ang).T[row]
    c[:, C_SIN:C_SIN + S] = np.sin(ang).T[row] * sign[:, None]
    c[:, C_BASE:C_BASE + E] = (CAP * np.arange(E) + 1)[None, :]
    p = np.arange(P)
    c[:, C_OWN:C_OWN + EG] = p[:, None] % EG == np.arange(EG)[None, :]
    c[:, C_HALF] = p % 32 < DK
    c[:, C_HALF + 1] = p % 32 >= DK
    c[p, C_PERM + p % EG * CAP + p // EG] = 1
    c[:, C_TRI:C_TRI + P] = p[:, None] < p[None, :]
    c[:, C_M1:C_M1 + P] = np.where(p[None, :] > p[:, None], f(-1e30), f(0))
    c[:, C_M2:C_M2 + P] = np.where(p[:, None] > p[None, :], f(-1e30), f(0))
    c[:, C_IDS:C_IDS + 2 * NC:2] = np.arange(NC)[None, :]
    c[:, C_IDS + 1:C_IDS + 2 * NC:2] = p[:, None]
    return c


_INS = ["L0_attn_x", "L0_attn_wq", "L0_attn_wk", "L0_attn_wv", "L0_attn_wo", "L0_ffn_gate_w", "L0_ffn_w_gate",
        "L0_ffn_w_up", "L0_ffn_w_down", "L0_ffn_sw_gate", "L0_ffn_sw_up", "L0_ffn_sw_down"]


def kernel(**inputs):
    import numpy as _np
    import concourse.bacc as _bacc
    from concourse.bass_utils import run_bass_kernel_spmd as _run

    nc = _bacc.Bacc("TRN2", target_bir_lowering=False, num_devices=1)
    arrays, args = {}, []
    for name in _INS + ["const"]:
        a = constants(_np) if name == "const" else _np.ascontiguousarray(inputs[name])
        arrays[f"in_{name}"] = a
        args.append(nc.dram_tensor(f"in_{name}", a.shape, F32, kind="ExternalInput").ap())
    out = nc.dram_tensor("out0", (B, S, D), F32, kind="ExternalOutput").ap()
    program(nc, *args, out)
    r = _run(nc, [arrays], core_ids=[0])
    return r.results[0]["out0"]
```
